# Optimizing a Trainium2 kernel written in Bass

```python
import numpy as np
import jax
import jax.numpy as jnp

def _softmax(x, axis=-1):
    return jax.nn.softmax(x, axis=axis)

def _gelu(x):
    return jax.nn.gelu(x, approximate=True)

def _silu(x):
    return jax.nn.silu(x)

def _sigmoid(x):
    return jax.nn.sigmoid(x)

def _layernorm(x, axis=-1, eps=1e-05):
    m = jnp.mean(x, axis=axis, keepdims=True)
    v = jnp.var(x, axis=axis, keepdims=True)
    return (x - m) / jnp.sqrt(v + eps)

def _scatter_add(tgt, idx, src, axis=0):
    return tgt.at[idx].add(src)

def _segment_sum(src, seg, n):
    return jax.ops.segment_sum(src, seg, n)
kernel_name = 'mk_gnn_preln_d2_gnn_r8_59d5f4'

def setup_inputs(seed: int=0):
    np.random.seed(seed)
    _w = jnp.asarray

    def _rec_inputs():
        import jax
        import jax.numpy as jnp
        _gk = jax.random.key(seed)
        x = -0.0002117 + 1 * jax.random.normal(jax.random.fold_in(_gk, 1), (1250, 512), jnp.float32)
        _s = jax.random.randint(jax.random.fold_in(_gk, 2), (10000,), 0, 1250, jnp.int32)
        _d = jax.random.randint(jax.random.fold_in(_gk, 3), (10000,), 0, 1250, jnp.int32)
        _loop = jnp.arange(1250, dtype=jnp.int32)
        src = jnp.concatenate([_s, _d, _loop])
        dst = jnp.concatenate([_d, _s, _loop])
        _o = jnp.argsort(dst, stable=True)
        src = src[_o]
        dst = dst[_o]
        edge_type_4 = jax.random.randint(jax.random.fold_in(_gk, 12), (21250,), 0, 4, jnp.int32)
        return (x, src, dst, edge_type_4)
    x, src, dst, edge_type_4 = _rec_inputs()

    def _L0_gnn_setup():
        import jax, jax.numpy as jnp
        import numpy as np
        N = 6250
        IN_CH = 512
        OUT_CH = 512
        DEG = 32
        E = N * DEG
        key = jax.random.key(seed)
        kx, kwc, kwn, kb, ke = jax.random.split(key, 5)
        x = jax.random.normal(kx, (N, IN_CH), dtype=jnp.float32)
        bound = 1.0 / np.sqrt(IN_CH)
        wc = jax.random.uniform(kwc, (IN_CH, OUT_CH), minval=-bound, maxval=bound, dtype=jnp.float32)
        wn = jax.random.uniform(kwn, (IN_CH, OUT_CH), minval=-bound, maxval=bound, dtype=jnp.float32)
        bias = jax.random.uniform(kb, (OUT_CH,), minval=-bound, maxval=bound, dtype=jnp.float32)
        src = jnp.repeat(jnp.arange(N, dtype=jnp.int64), DEG)
        dst = jax.random.randint(ke, (E,), 0, N, dtype=jnp.int64)
        edge_index = jnp.stack([src, dst], axis=0)
        return {'x': x, 'wc': wc, 'wn': wn, 'bias': bias, 'edge_index': edge_index}
    _L0_gnn_all = _L0_gnn_setup()
    _L0_gnn_in = {k: v for k, v in _L0_gnn_all.items() if k in ('wc', 'wn', 'bias')}
    del _L0_gnn_all

    def _L1_gnn_setup():
        import jax, jax.numpy as jnp
        import numpy as np
        N = 1250
        E = 20000
        DIM = 512
        R = 4
        EPS = 1e-05

        def layer_norm(h, w, b):
            mu = jnp.mean(h, axis=-1, keepdims=True)
            var = jnp.mean((h - mu) ** 2, axis=-1, keepdims=True)
            return (h - mu) * jax.lax.rsqrt(var + EPS) * w + b
        key = jax.random.key(seed)
        ks = jax.random.split(key, 12)
        s = 0.02
        inp = {'x': jax.random.normal(ks[0], (N, DIM), dtype=jnp.float32), 'edge_index': jax.random.randint(ks[1], (2, E), 0, N, dtype=jnp.int64), 'edge_type': jax.random.randint(ks[2], (E,), 0, R, dtype=jnp.int64), 'self_W': jax.random.normal(ks[3], (DIM, DIM), dtype=jnp.float32) * s, 'self_b': jnp.zeros((DIM,), dtype=jnp.float32), 'rel_W': jax.random.normal(ks[4], (R, DIM, DIM), dtype=jnp.float32) * s, 'rel_b': jnp.zeros((R, DIM), dtype=jnp.float32), 'ln1_w': jnp.ones((DIM,), dtype=jnp.float32), 'ln1_b': jnp.zeros((DIM,), dtype=jnp.float32), 'W1': jax.random.normal(ks[5], (DIM, 2 * DIM), dtype=jnp.float32) * s, 'b1': jnp.zeros((2 * DIM,), dtype=jnp.float32), 'W2': jax.random.normal(ks[6], (2 * DIM, DIM), dtype=jnp.float32) * s, 'b2': jnp.zeros((DIM,), dtype=jnp.float32), 'ln2_w': jnp.ones((DIM,), dtype=jnp.float32), 'ln2_b': jnp.zeros((DIM,), dtype=jnp.float32)}
        return inp
    _L1_gnn_all = _L1_gnn_setup()
    _L1_gnn_in = {k: v for k, v in _L1_gnn_all.items() if k in ('self_W', 'self_b', 'rel_W', 'rel_b', 'ln1_w', 'ln1_b', 'W1', 'b1', 'W2', 'b2', 'ln2_w', 'ln2_b')}
    del _L1_gnn_all
    return {'x': x, 'src': src, 'dst': dst, 'edge_type_4': edge_type_4, 'L0_gnn_wc': _L0_gnn_in['wc'], 'L0_gnn_wn': _L0_gnn_in['wn'], 'L0_gnn_bias': _L0_gnn_in['bias'], 'L1_gnn_self_W': _L1_gnn_in['self_W'], 'L1_gnn_self_b': _L1_gnn_in['self_b'], 'L1_gnn_rel_W': _L1_gnn_in['rel_W'], 'L1_gnn_rel_b': _L1_gnn_in['rel_b'], 'L1_gnn_ln1_w': _L1_gnn_in['ln1_w'], 'L1_gnn_ln1_b': _L1_gnn_in['ln1_b'], 'L1_gnn_W1': _L1_gnn_in['W1'], 'L1_gnn_b1': _L1_gnn_in['b1'], 'L1_gnn_W2': _L1_gnn_in['W2'], 'L1_gnn_b2': _L1_gnn_in['b2'], 'L1_gnn_ln2_w': _L1_gnn_in['ln2_w'], 'L1_gnn_ln2_b': _L1_gnn_in['ln2_b']}

def reference(x, src, dst, edge_type_4, L0_gnn_wc, L0_gnn_wn, L0_gnn_bias, L1_gnn_self_W, L1_gnn_self_b, L1_gnn_rel_W, L1_gnn_rel_b, L1_gnn_ln1_w, L1_gnn_ln1_b, L1_gnn_W1, L1_gnn_b1, L1_gnn_W2, L1_gnn_b2, L1_gnn_ln2_w, L1_gnn_ln2_b):
    import jax
    import jax.numpy as jnp

    def _L0_gnn_ref(x, wc, wn, bias, edge_index):
        import jax, jax.numpy as jnp
        import numpy as np
        N = 6250
        IN_CH = 512
        OUT_CH = 512
        DEG = 32
        E = N * DEG
        alpha = x @ wc
        beta = x @ wn
        src, dst = (edge_index[0], edge_index[1])
        sums = jax.ops.segment_sum(beta[dst], src, num_segments=x.shape[0])
        counts = jax.ops.segment_sum(jnp.ones_like(src, dtype=beta.dtype), src, num_segments=x.shape[0])
        gamma = sums / counts[:, None]
        return alpha + gamma + bias

    def _L1_gnn_ref(x, edge_index, edge_type, self_W, self_b, rel_W, rel_b, ln1_w, ln1_b, W1, b1, W2, b2, ln2_w, ln2_b):
        import jax, jax.numpy as jnp
        import numpy as np
        N = 1250
        E = 20000
        DIM = 512
        R = 4
        EPS = 1e-05

        def layer_norm(h, w, b):
            mu = jnp.mean(h, axis=-1, keepdims=True)
            var = jnp.mean((h - mu) ** 2, axis=-1, keepdims=True)
            return (h - mu) * jax.lax.rsqrt(var + EPS) * w + b
        n = x.shape[0]
        src, dst = (edge_index[0], edge_index[1])
        h_all = jnp.einsum('nd,rdf->nrf', x, rel_W) + rel_b
        msg = h_all[src, edge_type]
        agg = jax.ops.segment_sum(msg, dst, num_segments=n)
        deg = jax.ops.segment_sum(jnp.ones_like(dst, dtype=x.dtype), dst, num_segments=n)
        agg = agg / jnp.maximum(deg, 1.0)[:, None]
        h = x @ self_W + self_b + agg
        x1 = layer_norm(x + h, ln1_w, ln1_b)
        f = jax.nn.gelu(x1 @ W1 + b1, approximate=False) @ W2 + b2
        out = layer_norm(x1 + f, ln2_w, ln2_b)
        return out
    edge_index = jnp.stack([src, dst])
    h = jnp.maximum(_layernorm(x, axis=-1), 0.0)
    x = x + _L0_gnn_ref(h, L0_gnn_wc, L0_gnn_wn, L0_gnn_bias, edge_index)
    h = jnp.maximum(_layernorm(x, axis=-1), 0.0)
    x = x + _L1_gnn_ref(h, edge_index, edge_type_4, L1_gnn_self_W, L1_gnn_self_b, L1_gnn_rel_W, L1_gnn_rel_b, L1_gnn_ln1_w, L1_gnn_ln1_b, L1_gnn_W1, L1_gnn_b1, L1_gnn_W2, L1_gnn_b2, L1_gnn_ln2_w, L1_gnn_ln2_b)
    return x

_drawn_inputs = setup_inputs


def setup_inputs(seed=0):
    import zlib

    import numpy as np

    out = dict(_drawn_inputs(seed))
    spreads = {'L1_gnn_self_b': (0.0, 0.1),
     'L1_gnn_rel_b': (0.0, 0.1),
     'L1_gnn_ln1_w': (1.0, 0.2),
     'L1_gnn_ln1_b': (0.0, 0.1),
     'L1_gnn_b1': (0.0, 0.418),
     'L1_gnn_b2': (0.0, 0.1),
     'L1_gnn_ln2_w': (1.0, 0.2),
     'L1_gnn_ln2_b': (0.0, 0.1)}
    factors = {}
    for name, (base, spread) in spreads.items():
        noise = np.random.default_rng([zlib.crc32(name.encode()), seed]).standard_normal(out[name].shape)
        drawn = base * np.exp(spread * noise) if base else spread * noise
        out[name] = jnp.asarray(drawn.astype(out[name].dtype))
    for name, factor in factors.items():
        out[name] = (out[name] * factor).astype(out[name].dtype)
    return out
```

```python
import concourse.bass as bass
from concourse import mybir
from contextlib import ExitStack


def build_gnn(nc, x, src, dst, etype, wc, wn, bias0, self_w, self_b, rel_w, rel_b, ln1_w, ln1_b, w1, b1, w2, b2,
              ln2_w, ln2_b, out):
    fp32, fp16, i32 = mybir.dt.float32, mybir.dt.float16, mybir.dt.int32
    ALU, ACT, AX = mybir.AluOpType, mybir.ActivationFunctionType, mybir.AxisListType

    N, D = x.shape
    E = src.shape[0]
    R = rel_w.shape[0]
    F = w1.shape[1]
    P = 128
    EPS = 1e-5
    SPLIT = 2048.0
    NB = -(-N // P)
    KD = D // P
    KF = F // P
    rows = [min(P, N - b * P) for b in range(NB)]
    EP = 125
    EC = E // EP
    assert EP * EC == E and N < 2048 and R == 4

    NK = [NB, NB * R]
    GROUP = [2, 1]
    RING = 8
    STEP = 2 * RING
    bound = [(E + NK[l] * (GROUP[l] * P - 1)) // (GROUP[l] * P) * GROUP[l] for l in range(2)]
    STEPS = [-(-bound[l] // STEP) for l in range(2)]
    T = [STEP * STEPS[l] for l in range(2)]
    UNITS = [T[l] // GROUP[l] for l in range(2)]
    PS = STEPS[0]
    PC = -(-EC // PS)
    TM = max(T)
    NKM = max(NK)
    HALVES = [2 * s for s in STEPS]
    HBASE = [0, HALVES[0]]

    A0 = 0
    G0 = A0 + NB
    B0 = G0 + UNITS[0]
    S1 = B0 + NB
    G1 = S1 + NB
    R1 = G1 + UNITS[1]
    F1 = R1 + NB
    assert (UNITS[0] * 1) % 4 == 0 and UNITS[1] % 4 == 0
    GBASE = [G0, G1]

    node_groups = [list(range(g, min(g + 4, NB))) for g in range(0, NB, 4)]

    act_uses = [("t0", b) for b in range(NB)] + [("t1", b) for b in range(NB)]
    for g, blocks in enumerate(node_groups):
        act_uses += [("tx", b) for b in blocks] + [("w1", g, f) for f in range(KF)]
    act_at = {u: n for n, u in enumerate(act_uses)}

    tables = [nc.dram_tensor(f"gather_table_{l}", [N, 2 * D], fp16, kind="Internal").ap() for l in range(2)]

    ctx = ExitStack()
    with ctx:
        def sb(name, shape, dt=fp32):
            return ctx.enter_context(nc.sbuf_tensor(name, shape, dt))

        def ps(name, shape, dt=fp32):
            return ctx.enter_context(nc.psum_tensor(name, shape, dt))

        def sem(name):
            return ctx.enter_context(nc.semaphore(name))

        X = sb("X", [P, NB, D])
        H = sb("H", [P, NB, D])
        region = sb("region", [P, R * KD * D])
        HT = region[:, 0:KD * NB * P].rearrange("p (k n) -> p k n", k=KD)
        TSLOTS = (R * KD * D - KD * NB * P) // D
        parts = region[:, KD * NB * P:KD * NB * P + TSLOTS * D].bitcast(fp16).rearrange(
            "p (s t d) -> p s t d", s=TSLOTS, t=2)
        relw_sb = region[:, :].rearrange("p (r k n) -> p r k n", r=R, k=KD)
        gathered = sb("gathered", [P, RING, 2 * D], fp16)
        w1_sb = gathered[:, :, :].rearrange("p s n -> p (s n)").bitcast(fp32).rearrange("p (k n) -> p k n", k=KD)
        ACC = sb("ACC", [P, NKM, D])
        acc = [ACC[:, NKM - NB:NKM, :], ACC[:, :, :]]
        flat = ACC[:, 0:NKM - NB, :].rearrange("p k d -> p (k d)")
        half_words = NKM * EC // 2
        mask_all = flat[0:EP, 0:half_words].bitcast(fp16)
        seen_all = flat[0:EP, half_words:2 * half_words].bitcast(fp16)
        place_all = flat[0:EP, 2 * half_words:4 * half_words]
        onehot_words = PC * (P + 2 * TM) // 2
        onehots = flat[0:EP, 2 * half_words:2 * half_words + onehot_words].bitcast(fp16).rearrange(
            "p (c n) -> p c n", c=PC)
        wa = sb("wa", [P, KD, D])
        wb = sb("wb", [P, KD, D])
        segment_onehot = sb("segment_onehot", [P, 2, RING, P], fp16)
        rest = flat[0:EP, 4 * half_words:4 * half_words + 6 * EC + D]
        edges = rest[:, 0:3 * EC].bitcast(i32).rearrange("p (n j) -> p n j", n=3)
        int_a = rest[:, 3 * EC:4 * EC].bitcast(i32)
        int_b = rest[:, 4 * EC:5 * EC].bitcast(i32)
        block_f = rest[:, 5 * EC:6 * EC]
        bias_row = rest[0:1, 6 * EC:6 * EC + D]
        scal = sb("scal", [EP, PS * PC, 4])
        scal_now = sb("scal_now", [EP, PC, 4])
        last = sb("last", [EP, NKM], fp16)
        counts16 = sb("counts16", [EP, NKM], fp16)
        place0 = sb("place0", [EP, NKM])
        total_i = sb("total_i", [P, NKM], i32)
        units_f = sb("units_f", [P, 3, NKM])
        tiles_f = sb("tiles_f", [P, 2, NKM])
        reached = sb("reached", [P, 2, NKM])
        reached_b = sb("reached_b", [P, 2, NKM])
        tile_key = sb("tile_key", [P, 2, 2, NKM])
        unit_key = sb("unit_key", [P, 2])
        key_row = sb("key_row", [1, 2, 256], i32)
        gidx = sb("gidx", [P, TM], i32)
        gidx_now = sb("gidx_now", [P, 2, RING], i32)
        segrow = sb("segrow", [P, TM + RING])
        tile_counts = sb("tile_counts", [P, TM])
        tile_counts_t = sb("tile_counts_t", [P, 2, P])
        gtmp = tile_counts_t[:, :, :].rearrange("p a n -> p (a n)")
        count_k = sb("count_k", [NKM, P])
        count_m = sb("count_m", [NKM, 2, P])
        degree = sb("degree", [P, NB])
        inv = sb("inv", [P, 2, NB])
        stats = sb("stats", [P, NB, 6])
        mv = sb("mv", [P, NB, 2])
        std = sb("std", [P, NB])
        rstd = sb("rstd", [P, NB])
        b1_sb = sb("b1_sb", [P, KF])
        self_b_row = sb("self_b_row", [1, D])
        relb_sb = scal[0:NKM, :, :].rearrange("p j c -> p (j c)")[:, 0:D]
        ln1 = segment_onehot[:, :, :, :].rearrange("p a s n -> p (a s n)").bitcast(fp32).rearrange("p (a n) -> p a n", a=2)
        ln2w_sb, ln2b_sb, b2_row = ACC[:, 3, :], ACC[:, 7, :], ACC[0:1, 11, :]

        iota_col = sb("iota_col", [P, P])
        iota16 = sb("iota16", [P, TM], fp16)
        iota_key = sb("iota_key", [EP, NKM])
        index_p = sb("index_p", [P, 2])
        key_less = sb("key_less", [NKM, NB])
        key_ge = sb("key_ge", [NKM, NB])
        key_le = sb("key_le", [NKM, NB])
        key_block = sb("key_block", [NKM, NB])
        ident = sb("ident", [P, P])
        upper16 = sb("upper16", [P, P], fp16)
        ones16 = sb("ones16", [P, P], fp16)
        ones32 = sb("ones32", [1, P])
        one_col = sb("one_col", [P, 1])
        zeros16 = sb("zeros16", [P, 2 * TM], fp16)
        eps = sb("eps", [P, 1])

        ring = [ps(f"ring{n}", [P, D]) for n in range(4)]
        perm_ps = ps("perm_ps", [P, 512])
        small_ps = ps("small_ps", [P, 512])
        act_ps = [ps(f"act_ps{n}", [P, 512]) for n in range(2)]

        edges_in = sem("edges_in")
        x_in = [sem(f"x_in{b}") for b in range(NB)]
        wa_in, wb_in, relw_in, w1_in, w2_in = (sem(n) for n in ("wa_in", "wb_in", "relw_in", "w1_in", "w2_in"))
        rows_in, relb_in, ln1_in, late_in = (sem(n) for n in ("rows_in", "relb_in", "ln1_in", "late_in"))
        stored = [sem(f"stored{s}") for s in range(TSLOTS)]
        out_done = sem("out_done")
        pool_step, dve_step, act_step = sem("pool_step"), sem("dve_step"), sem("act_step")
        consts = sem("consts")
        ring_ready = sem("ring_ready")
        ring_free = sem("ring_free")
        act_ready, act_free = sem("act_ready"), sem("act_free")
        small_ready, small_free = sem("small_ready"), sem("small_free")
        perm_open = sem("perm_open")
        perm_ready = sem("perm_ready")
        perm_used, perm_done = sem("perm_used"), sem("perm_done")
        lists_ready = sem("lists_ready")
        stage_ready = sem("stage_ready")
        onehot_ready = sem("onehot_ready")
        tile_in = [sem(f"tile_in{s}") for s in range(RING)]
        slot_free = [sem(f"slot_free{s}") for s in range(RING)]
        counts_free = sem("counts_free")
        acc_clear = sem("acc_clear")
        var_ready, std_ready = sem("var_ready"), sem("std_ready")
        norm_ready = sem("norm_ready")
        relu_ready = sem("relu_ready")
        low_ready = sem("low_ready")
        stage_copied = sem("stage_copied")
        rel_counts = sem("rel_counts")
        x1_ready = sem("x1_ready")
        y_ready = sem("y_ready")

        block = ctx.enter_context(nc.Block())

        def hit(b):
            return [(k, slice(k * P, k * P + rows[b])) for k in range(KD)]

        def stores_of(s, layers):
            return layers * len(range(s, NB, TSLOTS))

        def gelu_out(f):
            v = ACC[:, :, :].rearrange("p (b r) d -> p b r d", r=R)
            return v[:, :, 1 + f // KD, (f % KD) * P:(f % KD + 1) * P]

        @block.sync
        def _(sp):
            for n, e in enumerate((src, dst, etype)):
                for lo, hi in ((0, 112), (112, EP)):
                    sp.dma_start(edges[lo:hi, n, :], e[lo * EC:hi * EC].rearrange("(p j) -> p j", j=EC)).then_inc(edges_in, 16)
            sp.wait_ge(consts, 1)
            for b in range(NB):
                sp.dma_start(X[0:rows[b], b, :], x[b * P:b * P + rows[b], :]).then_inc(x_in[b], 16)
            sp.dma_start(wa[:, :, :], wc.rearrange("(k p) n -> p k n", p=P)).then_inc(wa_in, 16)
            sp.dma_start(bias_row, bias0.rearrange("(a n) -> a n", a=1)).then_inc(rows_in, 16)
            sp.dma_start(self_b_row[0:1, :], self_b.rearrange("(a n) -> a n", a=1)).then_inc(rows_in, 16)
            sp.dma_start(b1_sb[:, :], b1.rearrange("(p k) -> p k", p=P)).then_inc(rows_in, 16)
            sp.dma_start(wb[:, :, :], wn.rearrange("(k p) n -> p k n", p=P)).then_inc(wb_in, 16)
            for l in range(2):
                for b in range(NB):
                    sp.wait_ge(relu_ready, l * NB + b + 1)
                    sp.wait_ge(low_ready, l * NB + b + 1)
                    s = b % TSLOTS
                    sp.dma_start(tables[l][b * P:b * P + rows[b], :],
                                 parts[0:rows[b], s].rearrange("p t d -> p (t d)")).then_inc(stored[s], 16)
                if l == 0:
                    sp.wait_ge(ring_ready, A0 + NB)
                    sp.dma_start(wa[:, :, :], self_w.rearrange("(k p) n -> p k n", p=P)).then_inc(wa_in, 16)
            for b in range(NB):
                sp.dma_start(relb_sb[R * b:R * b + R, :], rel_b).then_inc(relb_in, 16)
            sp.wait_ge(ring_ready, S1 + NB)
            for s in range(TSLOTS):
                sp.wait_ge(stored[s], 16 * stores_of(s, 2))
            sp.dma_start(relw_sb, rel_w.rearrange("r (k p) n -> p r k n", p=P)).then_inc(relw_in, 16)
            w2_v = w2.rearrange("(p k) n -> p k n", p=P)
            sp.dma_start(wa[:, :, :], w2_v[:, 0:KD, :]).then_inc(w2_in, 16)
            sp.dma_start(wb[:, :, :], w2_v[:, KD:KF, :]).then_inc(w2_in, 16)
            sp.wait_ge(ring_ready, G1 + UNITS[1])
            sp.wait_ge(slot_free[RING - 1], 1 + HALVES[0] + HALVES[1])
            sp.dma_start(ln1[:, 0, :], ln1_w.partition_broadcast(P)).then_inc(ln1_in, 16)
            sp.dma_start(ln1[:, 1, :], ln1_b.partition_broadcast(P)).then_inc(ln1_in, 16)
            sp.dma_start(w1_sb, w1.rearrange("(k p) n -> p k n", p=P)).then_inc(w1_in, 16)
            sp.wait_ge(ring_ready, R1 + 3)
            sp.dma_start(ln2w_sb, ln2_w.partition_broadcast(P)).then_inc(late_in, 16)
            sp.dma_start(ln2b_sb, ln2_b.partition_broadcast(P)).then_inc(late_in, 16)
            sp.dma_start(b2_row, b2.rearrange("(a n) -> a n", a=1)).then_inc(late_in, 16)
            for b in range(NB):
                sp.wait_ge(y_ready, b + 1)
                sp.dma_start(out[b * P:b * P + rows[b], :], X[0:rows[b], b, :]).then_inc(out_done, 16)
            sp.wait_ge(out_done, 16 * NB)

        @block.gpsimd
        def _(pool):
            nc.gpsimd.memset(X[:, NB - 1, :], 0.0).then_inc(consts, 1)
            nc.gpsimd.iota(iota16[:, :], [[1, TM]], base=0, channel_multiplier=0, allow_small_or_imprecise_dtypes=True)
            nc.gpsimd.iota(iota_col[:, :], [[1, P]], base=0, channel_multiplier=0, allow_small_or_imprecise_dtypes=True)
            nc.gpsimd.iota(iota_key[:, :], [[1, NKM]], base=0, channel_multiplier=0, allow_small_or_imprecise_dtypes=True)
            nc.gpsimd.iota(index_p[:, :], [[P, 2]], base=0, channel_multiplier=1, allow_small_or_imprecise_dtypes=True)
            nc.gpsimd.iota(key_less[:, :], [[-R, NB]], base=0, channel_multiplier=1, allow_small_or_imprecise_dtypes=True)
            nc.gpsimd.memset(ones16[:, :], 1.0)
            nc.gpsimd.memset(ones32[:, :], 1.0)
            nc.gpsimd.memset(one_col[:, :], 1.0)
            nc.gpsimd.memset(zeros16[:, :], 0.0)
            nc.gpsimd.memset(eps[:, :], EPS)
            nc.gpsimd.memset(scal[:, :, :], 0.0)
            nc.gpsimd.memset(segrow[:, :], 0.0).then_inc(consts, 1)
            nc.gpsimd.memset(acc[0], 0.0).then_inc(acc_clear, 1)
            nc.gpsimd.memset(gathered[:, :, :], 0.0).then_inc(pool_step, 1)
            pool.wait_ge(pool_step, 1)
            for s in range(RING):
                pool.sem_inc(slot_free[s], 1)
            last_row = pool.to_reg(N - 1)
            turn_regs = [pool.alloc_register(f"turn{h}") for h in range(2)]
            for l in range(2):
                if l == 1:
                    pool.wait_ge(ring_ready, B0 + NB)
                    pool.wait_ge(lists_ready, 2)
                    nc.gpsimd.memset(acc[1], 0.0).then_inc(acc_clear, 1)
                for s in range(TSLOTS):
                    pool.wait_ge(stored[s], 16 * stores_of(s, l + 1))
                with pool.Fori(0, STEPS[l]) as i:
                    turn = []
                    for h in range(2):
                        pool.reg_alu(turn_regs[h], i * 2, HBASE[l] + h + 1, ALU.add)
                        turn.append(pool.snap(turn_regs[h]))
                    for h in range(2):
                        for s in range(RING):
                            pool.wait_ge(stored[0], 16 * stores_of(0, l + 1))
                            pool.wait_ge(stage_ready, turn[h])
                            pool.wait_ge(slot_free[s], turn[h])
                            nc.gpsimd.indirect_dma_start(
                                gathered[:, s, :], None, tables[l],
                                bass.IndirectOffsetOnAxis(gidx_now[:, h, s:s + 1], 0),
                                bounds_check=last_row, oob_is_err=False).then_inc(tile_in[s], 16)

        @block.scalar
        def _(act):
            act.wait_ge(consts, 2)

            def square_roots(n):
                act.wait_ge(var_ready, n)
                nc.scalar.activation(std[:, :], mv[:, :, 1], ACT.Sqrt, bias=eps[:, 0:1]).then_inc(std_ready, 1)

            def relu_block(l, b):
                n = l * NB + b
                act.wait_ge(norm_ready, n + 1)
                nc.scalar.activation(H[:, b, :], H[:, b, :], ACT.Relu).then_inc(act_step, 1)
                s = b % TSLOTS
                if b >= TSLOTS or l:
                    act.wait_ge(stored[s], 16 * (stores_of(s, l) + b // TSLOTS))
                act.wait_ge(act_step, n + 1)
                nc.scalar.activation(parts[:, s, 0, :], H[:, b, :], ACT.Copy, scale=SPLIT).then_inc(relu_ready, 1)

            def copy_transposed(use, b, to):
                n = act_at[use]
                act.wait_ge(act_ready, n + 1)
                nc.scalar.copy(to, act_ps[n % 2][:, :].rearrange("p (k n) -> p k n", k=KD)[:, :, 0:rows[b]]
                               ).then_inc(act_free, 1)

            def copy_counts(l):
                with act.Fori(0, STEPS[l]) as i:
                    for h in range(2):
                        act.wait_ge(slot_free[RING - 1], i * 2 + (HBASE[l] + h + 2))
                        nc.scalar.copy(tile_counts[:, bass.ds(i * STEP + h * RING, RING)],
                                       act_ps[h][:, 0:RING]).then_inc(counts_free, 1)

            for l in range(2):
                for g in range(1):
                    square_roots(l + 1)
                for b in range(NB):
                    relu_block(l, b)
                    if b:
                        copy_transposed((f"t{l}", b - 1), b - 1, HT[:, :, (b - 1) * P:(b - 1) * P + rows[b - 1]])
                b = NB - 1
                copy_transposed((f"t{l}", b), b, HT[:, :, b * P:b * P + rows[b]])
                copy_counts(l)

            for b in range(NB):
                act.wait_ge(var_ready, 2 + b + 1)
                nc.scalar.activation(std[0:rows[b], b:b + 1], mv[0:rows[b], b, 1:2], ACT.Sqrt,
                                     bias=eps[0:rows[b], 0:1]).then_inc(std_ready, 1)
            act.wait_ge(rows_in, 48)
            for g, blocks in enumerate(node_groups):
                for b in blocks:
                    copy_transposed(("tx", b), b, ACC[:, R * b, :].rearrange("p (k n) -> p k n", k=KD)[:, :, 0:rows[b]])
                for f in range(KF):
                    n = act_at[("w1", g, f)]
                    act.wait_ge(act_ready, n + 1)
                    nb = len(blocks)
                    full = [b for b in blocks if rows[b] == P]
                    v = gelu_out(f)
                    c = 0
                    if len(full) > 0:
                        ins = nc.scalar.activation(v[:, full[0]:full[0] + len(full), :],
                                                   act_ps[n % 2][:, 0:len(full) * P].rearrange("p (b n) -> p b n", n=P),
                                                   ACT.Gelu, bias=b1_sb[:, f:f + 1])
                        c = len(full) * P
                    if len(full) < nb:
                        b = blocks[-1]
                        ins = nc.scalar.activation(v[:, b, 0:rows[b]], act_ps[n % 2][:, c:c + rows[b]],
                                                   ACT.Gelu, bias=b1_sb[:, f:f + 1])
                    ins.then_inc(act_free, 1)
            for b in range(NB):
                act.wait_ge(var_ready, 2 + NB + b + 1)
                nc.scalar.activation(std[0:rows[b], b:b + 1], mv[0:rows[b], b, 1:2], ACT.Sqrt,
                                     bias=eps[0:rows[b], 0:1]).then_inc(std_ready, 1)

        @block.vector
        def _(dve):
            steps = [0]

            def mark(ins):
                ins.then_inc(dve_step, 1)
                steps[0] += 1

            def done(ins):
                mark(ins)
                dve.wait_ge(dve_step, steps[0])

            def norm_stats(l):
                for b in range(NB):
                    if l == 0:
                        dve.wait_ge(x_in[b], 16)
                        if b == NB - 1:
                            dve.wait_ge(consts, 1)
                    mark(nc.vector.bn_stats(stats[:, b, :], X[:, b, :]))
                dve.wait_ge(dve_step, steps[0])
                for b in range(NB):
                    ins = nc.vector.bn_aggr(mv[:, b, :], stats[:, b, :])
                ins.then_inc(var_ready, 1)
                dve.wait_ge(std_ready, l + 1)
                done(nc.vector.reciprocal(rstd[:, :], std[:, :]))

            def low_part(l, b):
                s = b % TSLOTS
                dve.wait_ge(relu_ready, l * NB + b + 1)
                nc.vector.scalar_tensor_tensor(out=parts[:, s, 1, :], in0=H[:, b, :], scalar=SPLIT,
                                               in1=parts[:, s, 0, :], op0=ALU.mult, op1=ALU.subtract
                                               ).then_inc(low_ready, 1)

            def layer_norm(l):
                norm_stats(l)
                for b in range(NB):
                    nc.vector.tensor_scalar(H[:, b, :], X[:, b, :], mv[:, b, 0:1], rstd[:, b:b + 1],
                                            ALU.subtract, ALU.mult).then_inc(norm_ready, 1)
                    if b >= 2:
                        low_part(l, b - 2)
                for b in (NB - 2, NB - 1):
                    low_part(l, b)

            def rank(l):
                K = NK[l]
                seg, other = edges[:, l, :], edges[:, 1 - l, :]
                mask2, seen2 = mask_all[:, 0:K * EC], seen_all[:, 0:K * EC]
                mask = mask2.rearrange("p (k j) -> p k j", k=K)
                seen = seen2.rearrange("p (k j) -> p k j", k=K)
                place = place_all[:, 0:K * EC].rearrange("p (k j) -> p k j", k=K)
                shift = {1: 7, 2: 8}[GROUP[l]]
                done(nc.vector.tensor_scalar(int_a[:, :], seg, 7, None, ALU.logical_shift_right))
                if l == 0:
                    done(nc.vector.tensor_copy(block_f[:, :], int_a[:, :]))
                else:
                    done(nc.vector.scalar_tensor_tensor(out=block_f[:, :], in0=int_a[:, :], scalar=float(R),
                                                        in1=edges[:, 2, :], op0=ALU.mult, op1=ALU.add))
                mark(nc.vector.tensor_scalar(int_b[:, :], seg, 127, None, ALU.bitwise_and))
                mark(nc.vector.tensor_scalar(scal[:, 0:EC, 2], other, 1.0, None, ALU.add))
                done(nc.vector.tensor_tensor(mask, block_f[:, :].unsqueeze(1).to_broadcast([EP, K, EC]),
                                             iota_key[:, 0:K].unsqueeze(2).to_broadcast([EP, K, EC]), ALU.is_equal))
                mark(nc.vector.tensor_scalar(scal[:, 0:EC, 3], int_b[:, :], 1.0, None, ALU.add))
                done(nc.vector.tensor_tensor_scan(seen2, one_col[0:EP, 0:1].to_broadcast([EP, K * EC]), mask2, 0.0,
                                                  ALU.mult, ALU.add))
                done(nc.vector.tensor_copy(last[:, 0:K], seen[:, :, EC - 1]))
                mark(nc.vector.tensor_copy(counts16[:, 0:1], last[:, 0:1]))
                nc.vector.tensor_tensor(counts16[:, 1:K], last[:, 1:K], last[:, 0:K - 1], ALU.subtract).then_inc(
                    small_free, 1)
                dve.wait_ge(small_ready, 2 * l + 1)
                below, total = small_ps[0:EP, 0:K], small_ps[:, 64:64 + K]
                done(nc.vector.tensor_scalar(total_i[:, 0:K], total, float(GROUP[l] * P - 1), None, ALU.add))
                done(nc.vector.tensor_scalar(total_i[:, 0:K], total_i[:, 0:K], shift, None, ALU.logical_shift_right))
                done(nc.vector.tensor_copy(units_f[:, 0, 0:K], total_i[:, 0:K]))
                done(nc.vector.tensor_tensor_scan(units_f[:, 1, 0:K], one_col[:, 0:1].to_broadcast([P, K]),
                                                  units_f[:, 0, 0:K], 0.0, ALU.mult, ALU.add))
                done(nc.vector.tensor_tensor(units_f[:, 2, 0:K], units_f[:, 1, 0:K], units_f[:, 0, 0:K], ALU.subtract))
                done(nc.vector.scalar_tensor_tensor(out=place0[:, 0:K], in0=units_f[0:EP, 2, 0:K],
                                                    scalar=float(GROUP[l] * P), in1=below, op0=ALU.mult, op1=ALU.add))
                done(nc.vector.tensor_scalar(place0[:, 0:K], place0[:, 0:K], -1.0, None, ALU.add))
                done(nc.vector.tensor_tensor(place0[:, 1:K], place0[:, 1:K], last[:, 0:K - 1], ALU.subtract))
                done(nc.vector.tensor_tensor(place, seen, place0[:, 0:K].unsqueeze(2).to_broadcast([EP, K, EC]), ALU.add))
                done(nc.vector.tensor_tensor(place, place, mask, ALU.mult))
                done(nc.vector.tensor_reduce(block_f[:, :], place.rearrange("p k j -> p j k"), AX.X, ALU.add))
                done(nc.vector.tensor_copy(int_a[:, :], block_f[:, :]))
                mark(nc.vector.tensor_scalar(int_b[:, :], int_a[:, :], 7, None, ALU.logical_shift_right))
                done(nc.vector.tensor_scalar(int_a[:, :], int_a[:, :], 127, None, ALU.bitwise_and))
                mark(nc.vector.tensor_copy(scal[:, 0:EC, 0], int_a[:, :]))
                done(nc.vector.tensor_copy(scal[:, 0:EC, 1], int_b[:, :]))
                for n, m in ((0, 1), (1, 2)):
                    done(nc.vector.tensor_scalar(tiles_f[:, n, 0:K], units_f[:, m, 0:K], float(GROUP[l]), None, ALU.mult))
                for c in range(2):
                    at = index_p[:, c:c + 1]
                    mark(nc.vector.tensor_scalar(reached[:, c, 0:K], tiles_f[:, 1, 0:K], at, None, ALU.is_le))
                    done(nc.vector.tensor_scalar(reached_b[:, c, 0:K], tiles_f[:, 0, 0:K], at, None, ALU.is_le))
                    done(nc.vector.tensor_tensor(tile_key[:, l, c, 0:K], reached[:, c, 0:K], reached_b[:, c, 0:K],
                                                 ALU.subtract))
                    done(nc.vector.tensor_scalar(reached[:, c, 0:K], units_f[:, 1, 0:K], at, None, ALU.is_le))
                done(nc.vector.tensor_reduce(unit_key[:, :], reached[:, :, 0:K], AX.X, ALU.add))
                nc.vector.tensor_scalar(unit_key[:, :], unit_key[:, :], float(K - 1), None, ALU.min).then_inc(small_free, 1)
                dve.wait_ge(small_ready, 2 * l + 2)
                done(nc.vector.tensor_copy(key_row[0:1, l, :], small_ps[0:1, 0:256]))

            def permute_stage(l, i):
                dve.wait_ge(perm_ready, i * PC + (PS * PC * l + 1))
                nc.vector.tensor_copy(scal_now[:, :, :], scal[:, bass.ds(i * PC, PC), :]).then_inc(stage_copied, 1)
                dve.wait_ge(stage_copied, i + (PS * l + 1))

            def permute_column(l, i, c):
                v = scal_now[:, c, :]
                slot, byrow, byseg = (onehots[:, c, 0:P], onehots[:, c, P:P + T[l]], onehots[:, c, P + T[l]:P + 2 * T[l]])
                dve.wait_ge(perm_used, i * PC + (PS * PC * l + c + 1))
                nc.vector.tensor_scalar(slot, iota16[0:EP, 0:P], v[:, 0:1], None, ALU.is_equal)
                nc.vector.tensor_scalar(byrow, iota16[0:EP, 0:T[l]], v[:, 1:2], v[:, 2:3], ALU.is_equal, ALU.mult)
                nc.vector.tensor_scalar(byseg, iota16[0:EP, 0:T[l]], v[:, 1:2], v[:, 3:4], ALU.is_equal,
                                        ALU.mult).then_inc(perm_ready, 1)

            def lists(l):
                dve.wait_ge(perm_done, l + 1)
                done(nc.vector.tensor_scalar(gtmp[:, 0:T[l]], perm_ps[:, 0:T[l]], 0.0, 4096.0, ALU.is_equal, ALU.mult))
                mark(nc.vector.scalar_tensor_tensor(out=gidx[:, 0:T[l]], in0=perm_ps[:, 0:T[l]], scalar=-1.0,
                                                    in1=gtmp[:, 0:T[l]], op0=ALU.add, op1=ALU.add))
                done(nc.vector.tensor_scalar(segrow[:, 0:T[l]], perm_ps[:, T[l]:2 * T[l]], -1.0, None, ALU.add))
                nc.vector.sem_inc(lists_ready, 1)

            def make_onehot(l, q, at, buf):
                if not (isinstance(q, int) and q == 0):
                    dve.wait_ge(slot_free[RING - 1], q)
                nc.vector.tensor_tensor(segment_onehot[:, buf, :, :],
                                        iota_col[:, :].unsqueeze(1).to_broadcast([P, RING, P]),
                                        segrow[:, bass.ds(at, RING)].unsqueeze(2).to_broadcast([P, RING, P]),
                                        ALU.is_equal).then_inc(onehot_ready, 1)

            regs = [dve.alloc_register(f"key{u}") for u in range(STEP)]

            def gather(l):
                per_half = RING // GROUP[l]
                per_step = 2 * per_half
                make_onehot(l, HBASE[l], 0, 0)
                with dve.Fori(0, STEPS[l]) as i:
                    use = regs[0:per_step]
                    dve.load(use, key_row[0:1, l, bass.ds(i * per_step, per_step)])
                    keys = [dve.snap(r, min_val=0, max_val=NK[l] - 1) for r in use]
                    nc.vector.tensor_copy(gidx_now[:, 0, :], gidx[:, bass.ds(i * STEP, RING)]).then_inc(stage_ready, 1)
                    for h in range(2):
                        make_onehot(l, i * 2 + (HBASE[l] + h + 1), i * STEP + (h + 1) * RING, 1 - h)
                        if h == 0:
                            nc.vector.tensor_copy(gidx_now[:, 1, :], gidx[:, bass.ds(i * STEP + RING, RING)]
                                                  ).then_inc(stage_ready, 1)
                        if l == 0 and h == 0:
                            permute_stage(1, i)
                        for w in range(per_half):
                            u = h * per_half + w
                            n = i * per_step + (GBASE[l] + u + 1)
                            dve.wait_ge(ring_ready, n)
                            dve.wait_ge(ring_free, n + 3)
                            a = acc[l][:, bass.ds(keys[u], 1), :]
                            nc.vector.tensor_tensor(a, a, ring[(GBASE[l] + u) % 4][:, :].unsqueeze(1), ALU.add
                                                    ).then_inc(ring_free, 1)
                            if l == 0:
                                for c in range(2 * u, min(2 * u + 2, PC)):
                                    permute_column(1, i, c)

            def counts(l):
                K = NK[l]
                T1 = T[l] - P
                dve.wait_ge(small_ready, 2 * l + 5)
                mark(nc.vector.tensor_copy(tile_counts_t[:, 0, :], small_ps[:, 0:P]))
                nc.vector.tensor_copy(tile_counts_t[0:T1, 1, :], small_ps[0:T1, P:2 * P]).then_inc(small_free, 1)
                dve.wait_ge(small_ready, 2 * l + 6)
                if l == 0:
                    mark(nc.vector.memset(inv[:, 0, NB - 1:NB], 0.0))
                    mark(nc.vector.reciprocal(inv[:, 0, 0:NB - 1], small_ps[:, 0:NB - 1]))
                    dve.wait_ge(dve_step, steps[0])
                    done(nc.vector.reciprocal(inv[0:rows[NB - 1], 0, NB - 1:NB], small_ps[0:rows[NB - 1], NB - 1:NB]))
                else:
                    mark(nc.vector.tensor_copy(count_k[:, :], small_ps[0:K, 64:64 + P]))
                    done(nc.vector.tensor_reduce(degree[:, :], small_ps[:, 0:K].rearrange("p (b r) -> p b r", r=R),
                                                 AX.X, ALU.add))
                    done(nc.vector.tensor_scalar(degree[:, :], degree[:, :], 1.0, None, ALU.max))
                    done(nc.vector.reciprocal(inv[:, 1, :], degree[:, :]))
                done(nc.vector.tensor_scalar(inv[:, l, :], inv[:, l, :], 1.0 / SPLIT, None, ALU.mult))

            def final_norm(n, b, w, bb):
                r = rows[b]
                h = H[0:r, b, :]
                done(nc.vector.bn_stats(stats[0:r, b, :], h))
                nc.vector.bn_aggr(mv[0:r, b, :], stats[0:r, b, :]).then_inc(var_ready, 1)
                dve.wait_ge(std_ready, 2 + n * NB + b + 1)
                done(nc.vector.reciprocal(rstd[0:r, b:b + 1], std[0:r, b:b + 1]))
                done(nc.vector.tensor_scalar(h, h, mv[0:r, b, 0:1], rstd[0:r, b:b + 1], ALU.subtract, ALU.mult))
                done(nc.vector.tensor_tensor(h, h, w[0:r], ALU.mult))
                return nc.vector.tensor_tensor(h, h, bb[0:r], ALU.add)

            dve.wait_ge(consts, 2)
            mark(nc.vector.tensor_scalar(ident[:, :], iota_col[:, :], index_p[:, 0:1], None, ALU.is_equal))
            mark(nc.vector.tensor_scalar(upper16[:, :], iota_col[:, :], index_p[:, 0:1], None, ALU.is_gt))
            mark(nc.vector.tensor_scalar(key_ge[:, :], key_less[:, :], 0.0, SPLIT, ALU.is_ge, ALU.mult))
            done(nc.vector.tensor_scalar(key_le[:, :], key_less[:, :], float(R - 1), None, ALU.is_le))
            done(nc.vector.tensor_tensor(key_block[:, :], key_ge[:, :], key_le[:, :], ALU.mult))
            nc.vector.sem_inc(consts, 1)
            nc.vector.sem_inc(ring_free, 4)
            nc.vector.sem_inc(perm_ready, 1)

            layer_norm(0)
            dve.wait_ge(edges_in, 96)
            rank(0)
            with dve.Fori(0, PS) as i:
                permute_stage(0, i)
                for c in range(PC):
                    permute_column(0, i, c)
            lists(0)
            for b in range(NB):
                r = rows[b]
                dve.wait_ge(ring_ready, A0 + b + 1)
                nc.vector.tensor_tensor(X[0:r, b, :], X[0:r, b, :], ring[(A0 + b) % 4][0:r, :], ALU.add).then_inc(ring_free, 1)
            rank(1)
            dve.wait_ge(acc_clear, 1)
            gather(0)
            lists(1)
            counts(0)
            for b in range(NB):
                r = rows[b]
                dve.wait_ge(ring_ready, B0 + b + 1)
                nc.vector.scalar_tensor_tensor(out=X[0:r, b, :], in0=ring[(B0 + b) % 4][0:r, :], scalar=inv[0:r, 0, b:b + 1],
                                               in1=X[0:r, b, :], op0=ALU.mult, op1=ALU.add).then_inc(ring_free, 1)
            dve.wait_ge(ring_free, 4 + B0 + NB)
            layer_norm(1)
            for b in range(NB):
                r = rows[b]
                dve.wait_ge(ring_ready, S1 + b + 1)
                dve.wait_ge(low_ready, NB + b + 1)
                nc.vector.tensor_tensor(H[0:r, b, :], H[0:r, b, :], ring[(S1 + b) % 4][0:r, :], ALU.add).then_inc(ring_free, 1)
            dve.wait_ge(acc_clear, 2)
            gather(1)
            counts(1)

            def block_counts(b):
                nc.vector.tensor_scalar(count_m[:, b % 2, :], count_k[:, :], key_block[:, b:b + 1], None, ALU.mult
                                        ).then_inc(rel_counts, 1)

            block_counts(0)
            block_counts(1)
            dve.wait_ge(ln1_in, 32)
            for b in range(NB):
                r = rows[b]
                dve.wait_ge(ring_ready, R1 + b + 1)
                if b + 2 < NB:
                    block_counts(b + 2)
                nc.vector.scalar_tensor_tensor(out=H[0:r, b, :], in0=ring[(R1 + b) % 4][0:r, :], scalar=inv[0:r, 1, b:b + 1],
                                               in1=H[0:r, b, :], op0=ALU.mult, op1=ALU.add).then_inc(ring_free, 1)
                dve.wait_ge(ring_free, 4 + R1 + b + 1)
                final_norm(0, b, ln1[:, 0, :], ln1[:, 1, :]).then_inc(x1_ready, 1)
            dve.wait_ge(late_in, 48)
            for b in range(NB):
                r = rows[b]
                dve.wait_ge(ring_ready, F1 + b + 1)
                nc.vector.tensor_tensor(H[0:r, b, :], H[0:r, b, :], ring[(F1 + b) % 4][0:r, :], ALU.add).then_inc(ring_free, 1)
                dve.wait_ge(ring_free, 4 + F1 + b + 1)
                done(final_norm(1, b, ln2w_sb, ln2b_sb))
                nc.vector.tensor_tensor(X[0:r, b, :], X[0:r, b, :], H[0:r, b, :], ALU.add).then_inc(y_ready, 1)

        @block.tensor
        def _(pe):
            pe.wait_ge(consts, 3)

            def mm(*a, **k):
                return nc.tensor.matmul(*a, **k)

            def transposes(use, b, of, ready, value):
                n = act_at[use]
                pe.wait_ge(ready, value)
                if n >= 2:
                    pe.wait_ge(act_free, n - 1)
                for k, cols in hit(b):
                    ins = nc.tensor.transpose(act_ps[n % 2][:, cols], of[0:rows[b], b, k * P:(k + 1) * P],
                                              ident[0:rows[b], 0:rows[b]])
                ins.then_inc(act_ready, 1)

            def node_product(n, b, terms, extra=None):
                pe.wait_ge(ring_free, n + 1)
                todo = list(terms) + ([extra] if extra else [])
                for m, (left, right) in enumerate(todo):
                    ins = mm(ring[n % 4][0:rows[b], :], left, right, start=(m == 0), stop=(m == len(todo) - 1))
                ins.then_inc(ring_ready, 1)

            def h_blocks(b, w):
                return [(HT[:, k, b * P:b * P + rows[b]], w[:, k, :]) for k in range(KD)]

            def rank_counts(l):
                K = NK[l]
                pe.wait_ge(small_free, 2 * l + 1)
                mm(small_ps[0:EP, 0:K], upper16[0:EP, 0:EP], counts16[:, 0:K], start=True, stop=True)
                mm(small_ps[:, 64:64 + K], ones16[0:EP, :], counts16[:, 0:K], start=True, stop=True).then_inc(small_ready, 1)

            def key_rows(l):
                pe.wait_ge(small_free, 2 * l + 2)
                for c in range(2):
                    ins = mm(small_ps[0:1, c * P:(c + 1) * P], unit_key[:, c:c + 1], ident[:, :], start=True, stop=True)
                ins.then_inc(small_ready, 1)

            def permute_open(l):
                if l:
                    pe.wait_ge(lists_ready, l)
                mm(perm_ps[:, 0:2 * T[l]], zeros16[0:EP, 0:P], zeros16[0:EP, 0:2 * T[l]], start=True, stop=False)

            def permute_column(l, i, c):
                pe.wait_ge(perm_ready, i * PC + (PS * PC * l + c + 2))
                mm(perm_ps[:, 0:2 * T[l]], onehots[:, c, 0:P], onehots[:, c, P:P + 2 * T[l]], start=False,
                   stop=False).then_inc(perm_used, 1)

            def permute_close(l):
                mm(perm_ps[:, 0:2 * T[l]], zeros16[0:EP, 0:P], zeros16[0:EP, 0:2 * T[l]], start=False,
                   stop=True).then_inc(perm_done, 1)

            def gather(l):
                g = GROUP[l]
                with pe.Fori(0, STEPS[l]) as i:
                    half = [pe.snap(i * 2 + (HBASE[l] + h + 1)) for h in range(2)]
                    arrived = [pe.snap(i * 32 + 16 * (HBASE[l] + h + 1)) for h in range(2)]
                    c = 0
                    for h in range(2):
                        pe.wait_ge(onehot_ready, half[h] + l)
                        pe.wait_ge(counts_free, half[h])
                        for w in range(RING // g):
                            u = h * (RING // g) + w
                            slots = range(w * g, w * g + g)
                            for s in slots:
                                pe.wait_ge(tile_in[s], arrived[h])
                            pe.wait_ge(ring_free, i * (STEP // g) + (GBASE[l] + u + 1))
                            bank = ring[(GBASE[l] + u) % 4]
                            for k in range(KD):
                                m = 0
                                for s in slots:
                                    for part in range(2):
                                        ins = mm(bank[:, k * P:(k + 1) * P],
                                                 gathered[:, s, part * D + k * P:part * D + (k + 1) * P],
                                                 segment_onehot[:, h, s, :], start=(m == 0), stop=(m == 2 * g - 1))
                                        m += 1
                            ins.then_inc(ring_ready, 1)
                            for s in slots:
                                mm(act_ps[h][:, s:s + 1], segment_onehot[:, h, s, :], ones16[:, 0:1], start=True,
                                   stop=True).then_inc(slot_free[s], 1)
                            if l == 0:
                                for cc in range(2 * u, min(2 * u + 2, PC)):
                                    permute_column(1, i, cc)

            def counts(l):
                K = NK[l]
                T1 = T[l] - P
                pe.wait_ge(counts_free, 2 + sum(HALVES[:l + 1]))
                nc.tensor.transpose(small_ps[:, 0:P], tile_counts[:, 0:P], ident[:, :])
                nc.tensor.transpose(small_ps[0:T1, P:2 * P], tile_counts[:, P:T[l]], ident[:, :]).then_inc(small_ready, 1)
                pe.wait_ge(small_free, l + 5)
                for out_, left, right in ((small_ps[:, 0:K], 0, 1), (small_ps[0:K, 64:64 + P], 1, 0)):
                    for c, t in ((0, P), (1, T1)):
                        both = (tile_counts_t[0:t, c, :], tile_key[0:t, l, c, 0:K])
                        ins = mm(out_, both[left], both[right], start=(c == 0), stop=(c == 1))
                ins.then_inc(small_ready, 1)

            for l in range(1):
                for b in range(NB):
                    transposes(("t0", b), b, H, relu_ready, b + 1)
            pe.wait_ge(wa_in, 16)
            pe.wait_ge(rows_in, 48)

            def alpha(blocks):
                for b in blocks:
                    pe.wait_ge(act_free, act_at[("t0", b)] + 1)
                    node_product(A0 + b, b, h_blocks(b, wa), (ones32[0:1, 0:rows[b]], bias_row))

            alpha(range(4))
            rank_counts(0)
            key_rows(0)
            pe.sem_inc(perm_used, PC)
            pe.sem_inc(counts_free, 2)
            permute_open(0)
            with pe.Fori(0, PS) as i:
                for c in range(PC):
                    permute_column(0, i, c)
            permute_close(0)
            alpha(range(4, NB))
            rank_counts(1)
            key_rows(1)
            permute_open(1)
            gather(0)
            permute_close(1)
            counts(0)
            pe.wait_ge(wb_in, 16)
            pe.wait_ge(ring_free, 4 + B0)
            for b in range(NB):
                node_product(B0 + b, b, [(acc[0][:, b, k * P:k * P + rows[b]], wb[:, k, :]) for k in range(KD)])
            for b in range(NB):
                transposes(("t1", b), b, H, relu_ready, NB + b + 1)
            pe.wait_ge(wa_in, 32)
            for b in range(NB):
                pe.wait_ge(act_free, act_at[("t1", b)] + 1)
                node_product(S1 + b, b, h_blocks(b, wa), (ones32[0:1, 0:rows[b]], self_b_row[0:1, :]))
            gather(1)
            counts(1)
            pe.wait_ge(relw_in, 16)
            pe.wait_ge(relb_in, 16 * NB)
            pe.wait_ge(ring_free, 4 + R1)
            for b in range(NB):
                pe.wait_ge(rel_counts, b + 1)
                node_product(R1 + b, b, [(ACC[:, R * b + r, k * P:k * P + rows[b]], relw_sb[:, r, k, :])
                                         for r in range(R) for k in range(KD)],
                             (count_m[:, b % 2, 0:rows[b]], relb_sb[:, :]))
            pe.wait_ge(w1_in, 16)
            for g, blocks in enumerate(node_groups):
                for b in blocks:
                    transposes(("tx", b), b, H, x1_ready, b + 1)
                pe.wait_ge(act_free, act_at[("tx", blocks[-1])] + 1)
                for f in range(KF):
                    n = act_at[("w1", g, f)]
                    pe.wait_ge(act_free, n - 1)
                    full = [b for b in blocks if rows[b] == P]
                    spans = [(full[0], len(full), P)] if full else []
                    spans += [(b, 1, rows[b]) for b in blocks if rows[b] < P]
                    at = 0
                    for b, nb, r in spans:
                        for k in range(KD):
                            xt = ACC[:, :, :].rearrange("p (b r) d -> p b r d", r=R)[:, b:b + nb, 0, k * P:k * P + r]
                            ins = mm(act_ps[n % 2][:, at:at + nb * r], w1_sb[:, k, f::KF], xt,
                                     start=(k == 0), stop=(k == KD - 1))
                        at += nb * r
                    ins.then_inc(act_ready, 1)
            pe.wait_ge(w2_in, 32)
            pe.wait_ge(late_in, 48)
            for g, blocks in enumerate(node_groups):
                pe.wait_ge(act_free, act_at[("w1", g, KF - 1)] + 1)
                for b in blocks:
                    node_product(F1 + b, b, [(gelu_out(f)[:, b, 0:rows[b]], (wa, wb)[f // KD][:, f % KD, :])
                                             for f in range(KF)], (ones32[0:1, 0:rows[b]], b2_row))


_INS = ['x', 'src', 'dst', 'edge_type_4', 'L0_gnn_wc', 'L0_gnn_wn', 'L0_gnn_bias', 'L1_gnn_self_W', 'L1_gnn_self_b',
        'L1_gnn_rel_W', 'L1_gnn_rel_b', 'L1_gnn_ln1_w', 'L1_gnn_ln1_b', 'L1_gnn_W1', 'L1_gnn_b1', 'L1_gnn_W2',
        'L1_gnn_b2', 'L1_gnn_ln2_w', 'L1_gnn_ln2_b']


def kernel(**inputs):
    import numpy as _np
    import concourse.bacc as _bacc
    from concourse import mybir as _mybir
    from concourse.bass_utils import run_bass_kernel_spmd as _run

    nc = _bacc.Bacc("TRN2", target_bir_lowering=False, num_devices=1)
    arrays, args = {}, []
    for name in _INS:
        a = _np.ascontiguousarray(inputs[name])
        arrays[f"in_{name}_dram"] = a
        args.append(nc.dram_tensor(f"in_{name}_dram", a.shape, _mybir.dt.from_np(a.dtype), kind="ExternalInput").ap())
    shape = inputs['x'].shape
    args.append(nc.dram_tensor("out_0_dram", shape, _mybir.dt.float32, kind="ExternalOutput").ap())
    build_gnn(nc, *args)
    r = _run(nc, [arrays], core_ids=[0])
    return r.results[0]["out_0_dram"]
```

```python
import concourse.bass as bass
from concourse import mybir
from contextlib import ExitStack


def build_gnn(nc, x, src, dst, etype, wc, wn, bias0, self_w, self_b, rel_w, rel_b, ln1_w, ln1_b, w1, b1, w2, b2,
              ln2_w, ln2_b, out):
    fp32, fp16, i32 = mybir.dt.float32, mybir.dt.float16, mybir.dt.int32
    ALU, ACT, AX = mybir.AluOpType, mybir.ActivationFunctionType, mybir.AxisListType

    N, D = x.shape
    E = src.shape[0]
    R = rel_w.shape[0]
    F = w1.shape[1]
    P = 128
    EPS = 1e-5
    SPLIT = 2048.0
    TYPE_AT = 8
    NB = -(-N // P)
    KD = D // P
    KF = F // P
    rows = [min(P, N - b * P) for b in range(NB)]
    EP = 125
    EC = E // EP
    assert EP * EC == E and N < 2048 and (R - 1) * 2 ** TYPE_AT + P < 2048

    RING = 8
    STEP = 2 * RING
    STEPS = -(-((E + NB * (P - 1)) // P) // STEP)
    T = STEP * STEPS
    HALVES = 2 * STEPS
    assert T >= EC and 2 * T <= 512

    G0 = 0
    B0 = G0 + T
    M1 = B0 + NB
    S1 = M1 + NB * R
    G1 = S1 + NB
    F1 = G1 + T
    GBASE = [G0, G1]

    node_groups = [list(range(g, min(g + 4, NB))) for g in range(0, NB, 4)]

    act_uses = [("t0", 0)]
    EARLY = 5
    for b in range(NB):
        act_uses += [("t0", b + 1)] * (b + 1 < NB) + [("a0", b)] * (b < EARLY)
    act_uses += [("a0", b) for b in range(EARLY, NB)] + [("t1", b) for b in range(NB)]
    for g, blocks in enumerate(node_groups):
        act_uses += [("tx", b) for b in blocks] + [("w1", g, f) for f in range(KF)]
    act_at = {u: n for n, u in enumerate(act_uses)}

    h0_table = nc.dram_tensor("h0_table", [N, 2 * D], fp16, kind="Internal").ap()
    message_table = nc.dram_tensor("message_table", [N, R * D], fp32, kind="Internal").ap()
    gather_from = [h0_table, message_table.rearrange("n (r d) -> (n r) d", r=R)]
    last_row = [N - 1, N * R - 1]

    ctx = ExitStack()
    with ctx:
        def sb(name, shape, dt=fp32):
            return ctx.enter_context(nc.sbuf_tensor(name, shape, dt))

        def ps(name, shape, dt=fp32):
            return ctx.enter_context(nc.psum_tensor(name, shape, dt))

        def sem(name):
            return ctx.enter_context(nc.semaphore(name))

        X = sb("X", [P, NB, D])
        H = sb("H", [P, NB, D])
        HT = sb("HT", [P, NB, KD, P])
        ACC = sb("ACC", [P, NB, D])
        tiles = sb("tiles", [P, RING * D + 2 * RING * P])
        gathered = tiles[:, 0:RING * D].rearrange("p (s n) -> p s n", s=RING)
        gathered16 = tiles[:, 0:RING * D].bitcast(fp16).rearrange("p (s n) -> p s n", s=RING)
        segment_onehot = tiles[:, RING * D:].rearrange("p (h s n) -> p h s n", h=2, s=RING)
        segment_onehot16 = tiles[:, RING * D:RING * D + RING * P].bitcast(fp16).rearrange(
            "p (h s n) -> p h s n", h=2, s=RING)
        assert KF == 2 * KD and RING * D + 2 * RING * P >= NB * D
        gelu_parts = [v.rearrange("p (b c n) -> p b c n", b=NB, c=KD)
                      for v in (ACC[:, :, :].rearrange("p b d -> p (b d)"), tiles[:, 0:NB * D])]
        region = sb("region", [P, R * KD * D])
        relw_sb = region[:, :].rearrange("p (r k n) -> p r k n", r=R, k=KD)
        w1_sb = region[:, 0:KD * F].rearrange("p (k n) -> p k n", k=KD)
        w2_sb = region[:, KD * F:KD * F + KF * D].rearrange("p (k n) -> p k n", k=KF)
        cut = [0]

        def scratch(words):
            cut[0] += words
            return region[0:EP, cut[0] - words:cut[0]]

        mask2 = scratch(NB * EC // 2).bitcast(fp16)
        seen2 = scratch(NB * EC // 2).bitcast(fp16)
        mask = mask2.rearrange("p (k j) -> p k j", k=NB)
        seen = seen2.rearrange("p (k j) -> p k j", k=NB)
        place = scratch(NB * EC).rearrange("p (k j) -> p k j", k=NB)
        slot_onehot, row_onehot, seg_onehot = (
            scratch(P * STEP // 2).bitcast(fp16).rearrange("p (h n j) -> p h n j", h=2, j=RING) for _ in range(3))
        tile_onehot = scratch(T * STEP // 2).bitcast(fp16).rearrange("p (h n j) -> p h n j", h=2, j=RING)
        assert cut[0] <= R * KD * D

        OUTS = 3
        out_slots = sb("out_slots", [P, OUTS, 2, D])
        parts = out_slots[:, :, :, :].rearrange("p s t d -> p (s t d)").bitcast(fp16).rearrange(
            "p (s t d) -> p s t d", s=2 * OUTS, t=2)
        PARTS = 2 * OUTS
        wa = sb("wa", [P, KD, D])
        wb = sb("wb", [P, KD, D])
        relb_sb = sb("relb_sb", [P, R, D])
        ln1, ln2 = sb("ln1", [P, 2, D]), sb("ln2", [P, 2, D])
        b2_sb = sb("b2_sb", [P, D])
        b1_sb = sb("b1_sb", [P, KF])
        bias_rows = sb("bias_rows", [1, 2, D])

        edges = sb("edges", [EP, 3, EC], i32)
        int_a = sb("int_a", [EP, EC], i32)
        int_b = sb("int_b", [EP, EC], i32)
        edge_f = sb("edge_f", [EP, EC])
        edge_data = sb("edge_data", [EP, 4, T], fp16)
        last = sb("last", [EP, NB], fp16)
        counts16 = sb("counts16", [EP, NB], fp16)
        place0 = sb("place0", [EP, NB])
        total_i = sb("total_i", [P, NB], i32)
        tiles_of = sb("tiles_of", [P, 3, NB])
        reached = sb("reached", [P, 2, 2, NB])
        tile_key = sb("tile_key", [P, 2, 2, NB])
        key_col = sb("key_col", [P, 2])
        key_row = sb("key_row", [1, 2, 2 * P], i32)
        gidx = sb("gidx", [P, T + RING], i32)
        gather_f = sb("gather_f", [P, 2, T])
        payload_i = sb("payload_i", [P, 2, T], i32)
        gidx_now = sb("gidx_now", [P, 2, RING], i32)
        segrow = sb("segrow", [P, T + RING])
        tile_counts = sb("tile_counts", [P, T])
        tile_counts_t = sb("tile_counts_t", [P, 2, P])
        inv = sb("inv", [P, 2, NB])
        stats = sb("stats", [P, NB, 6])
        mv = sb("mv", [P, NB, 2])
        std = sb("std", [P, NB])
        rstd = sb("rstd", [P, NB])

        iota_col = sb("iota_col", [P, P])
        iota_rep = sb("iota_rep", [P, T, RING], fp16)
        iota_key = sb("iota_key", [EP, NB])
        index_p = sb("index_p", [P, 2])
        ident = sb("ident", [P, P])
        upper16 = sb("upper16", [P, P], fp16)
        ones16 = sb("ones16", [P, P], fp16)
        ones32 = sb("ones32", [P, P])
        zeros16 = sb("zeros16", [P, 2 * T], fp16)
        eps = sb("eps", [P, 1])

        ring = [ps(f"ring{n}", [P, D]) for n in range(4)]
        perm_ps = ps("perm_ps", [P, 512])
        small_ps = ps("small_ps", [P, 512])
        act_ps = [ps(f"act_ps{n}", [P, 512]) for n in range(2)]

        edges_in = sem("edges_in")
        x_in = [sem(f"x_in{b}") for b in range(NB)]
        wa_in, wb_in, relw_in, w1_in, w2_in = (sem(n) for n in ("wa_in", "wb_in", "relw_in", "w1_in", "w2_in"))
        rows_in = sem("rows_in")
        parts_out = [sem(f"parts_out{s}") for s in range(PARTS)]
        messages_out = [sem(f"messages_out{s}") for s in range(OUTS)]
        out_done = sem("out_done")
        pool_step, dve_step, act_step = sem("pool_step"), sem("dve_step"), sem("act_step")
        consts = sem("consts")
        ring_ready = sem("ring_ready")
        ring_free = sem("ring_free")
        act_ready, act_free = sem("act_ready"), sem("act_free")
        small_ready, small_free = sem("small_ready"), sem("small_free")
        perm_ready = sem("perm_ready")
        slot_made = sem("slot_made")
        perm_used, perm_done = sem("perm_used"), sem("perm_done")
        lists_ready = sem("lists_ready")
        stage_ready = sem("stage_ready")
        onehot_ready = sem("onehot_ready")
        tile_in = [sem(f"tile_in{s}") for s in range(RING)]
        slot_free = [sem(f"slot_free{s}") for s in range(RING)]
        counts_free = sem("counts_free")
        acc_clear = sem("acc_clear")
        acc_used = sem("acc_used")
        var_ready, std_ready = sem("var_ready"), sem("std_ready")
        norm_ready = sem("norm_ready")
        relu_ready = sem("relu_ready")
        low_ready = sem("low_ready")
        message_ready = sem("message_ready")
        x1_ready = sem("x1_ready")
        y_ready = sem("y_ready")

        block = ctx.enter_context(nc.Block())

        def uses_of(s, slots, upto):
            return len(range(s, upto, slots))

        ROWS = 4 + R + 4

        def spans(blocks):
            full = [b for b in blocks if rows[b] == P]
            return [(full[0], len(full), P)] * bool(full) + [(b, 1, rows[b]) for b in blocks if rows[b] < P]

        def gelu_out(f, blocks):
            return gelu_parts[f // KD][:, blocks, f % KD, :]

        @block.sync
        def _(sp):
            for n, e in enumerate((src, dst, etype)):
                for lo, hi in ((0, 112), (112, EP)):
                    sp.dma_start(edges[lo:hi, n, :], e[lo * EC:hi * EC].rearrange("(p j) -> p j", j=EC)
                                 ).then_inc(edges_in, 16)
            sp.wait_ge(consts, 1)
            for b in range(NB):
                sp.dma_start(X[0:rows[b], b, :], x[b * P:b * P + rows[b], :]).then_inc(x_in[b], 16)
            sp.dma_start(wa[:, :, :], wc.rearrange("(k p) n -> p k n", p=P)).then_inc(wa_in, 16)
            for n, v in enumerate((bias0, self_b)):
                sp.dma_start(bias_rows[0:1, n, :], v.rearrange("(a n) -> a n", a=1)).then_inc(rows_in, 16)
            sp.dma_start(b1_sb[:, :], b1.rearrange("(p k) -> p k", p=P)).then_inc(rows_in, 16)
            sp.dma_start(b2_sb[:, :], b2.partition_broadcast(P)).then_inc(rows_in, 16)
            for r in range(R):
                sp.dma_start(relb_sb[:, r, :], rel_b[r, :].partition_broadcast(P)).then_inc(rows_in, 16)
            for to, vectors in ((ln1, (ln1_w, ln1_b)), (ln2, (ln2_w, ln2_b))):
                for n, v in enumerate(vectors):
                    sp.dma_start(to[:, n, :], v.partition_broadcast(P)).then_inc(rows_in, 16)
            sp.dma_start(wb[:, :, :], wn.rearrange("(k p) n -> p k n", p=P)).then_inc(wb_in, 16)
            for b in range(NB):
                sp.wait_ge(relu_ready, b + 1)
                sp.wait_ge(low_ready, b + 1)
                sp.dma_start(h0_table[b * P:b * P + rows[b], :],
                             parts[0:rows[b], b % PARTS].rearrange("p t d -> p (t d)")
                             ).then_inc(parts_out[b % PARTS], 16)
            sp.wait_ge(act_ready, act_at[("a0", NB - 1)] + 1)
            sp.dma_start(wa[:, :, :], self_w.rearrange("(k p) n -> p k n", p=P)).then_inc(wa_in, 16)
            sp.wait_ge(lists_ready, 2)
            sp.dma_start(relw_sb, rel_w.rearrange("r (k p) n -> p r k n", p=P)).then_inc(relw_in, 16)
            for n in range(NB * R // 2):
                b, pair = divmod(n, R // 2)
                sp.wait_ge(message_ready, n + 1)
                sp.dma_start(message_table[b * P:b * P + rows[b], pair * 2 * D:(pair + 1) * 2 * D],
                             out_slots[0:rows[b], n % OUTS].rearrange("p t d -> p (t d)")
                             ).then_inc(messages_out[n % OUTS], 16)
            sp.wait_ge(ring_ready, S1)
            sp.dma_start(w1_sb, w1.rearrange("(k p) n -> p k n", p=P)).then_inc(w1_in, 16)
            sp.dma_start(w2_sb, w2.rearrange("(p k) n -> p k n", p=P)).then_inc(w2_in, 16)
            for b in range(NB):
                sp.wait_ge(y_ready, b + 1)
                sp.dma_start(out[b * P:b * P + rows[b], :], X[0:rows[b], b, :]).then_inc(out_done, 16)
            sp.wait_ge(out_done, 16 * NB)

        @block.gpsimd
        def _(pool):
            def iota(to, pattern, channel_multiplier):
                nc.gpsimd.iota(to, pattern, base=0, channel_multiplier=channel_multiplier,
                               allow_small_or_imprecise_dtypes=True)

            nc.gpsimd.memset(X[:, NB - 1, :], 0.0).then_inc(consts, 1)
            nc.gpsimd.memset(eps[:, :], EPS)
            iota(iota_col[:, :], [[1, P]], 0)
            iota(iota_key[:, :], [[1, NB]], 0)
            iota(index_p[:, :], [[P, 2]], 1)
            nc.gpsimd.memset(edge_data[:, :, :], 0.0)
            nc.gpsimd.memset(ones16[:, :], 1.0)
            nc.gpsimd.memset(ones32[:, :], 1.0).then_inc(consts, 1)
            iota(iota_rep[:, :, :], [[1, T], [0, RING]], 0)
            nc.gpsimd.memset(zeros16[:, :], 0.0)
            nc.gpsimd.memset(gidx[:, :], 0)
            nc.gpsimd.memset(segrow[:, :], -1.0).then_inc(consts, 1)
            nc.gpsimd.memset(ACC[:, :, :], 0.0).then_inc(acc_clear, 1)
            nc.gpsimd.memset(gathered[:, :, :], 0.0).then_inc(pool_step, 1)
            pool.wait_ge(pool_step, 1)
            for s in range(RING):
                pool.sem_inc(slot_free[s], 1)
            limits = [pool.to_reg(last_row[l]) for l in range(2)]
            turn_regs, staged_regs = ([pool.alloc_register(f"{name}{h}") for h in range(2)] for name in ("turn", "staged"))
            for l in range(2):
                if l == 0:
                    table = [(parts_out[s], 16 * uses_of(s, PARTS, NB)) for s in range(PARTS)]
                else:
                    pool.wait_ge(ring_ready, M1)
                    nc.gpsimd.memset(ACC[:, :, :], 0.0).then_inc(acc_clear, 1)
                    table = [(messages_out[s], 16 * uses_of(s, OUTS, NB * R // 2)) for s in range(OUTS)]
                for s, value in table:
                    pool.wait_ge(s, value)
                with pool.Fori(0, STEPS) as i:
                    turn, staged = [], []
                    for h in range(2):
                        pool.reg_alu(turn_regs[h], i * 2, l * HALVES + h + 1, ALU.add)
                        turn.append(pool.snap(turn_regs[h]))
                        pool.reg_alu(staged_regs[h], i * 2, l * (HALVES + 1) + h + 1, ALU.add)
                        staged.append(pool.snap(staged_regs[h]))
                    for h in range(2):
                        for s in range(RING):
                            pool.wait_ge(*table[0])
                            pool.wait_ge(stage_ready, staged[h])
                            pool.wait_ge(slot_free[s], turn[h])
                            nc.gpsimd.indirect_dma_start(
                                (gathered16, gathered)[l][:, s, :], None, gather_from[l],
                                bass.IndirectOffsetOnAxis(gidx_now[:, h, s:s + 1], 0),
                                bounds_check=limits[l], oob_is_err=False).then_inc(tile_in[s], 16)

        @block.scalar
        def _(act):
            roots = [0]
            act.wait_ge(consts, 2)

            def square_root(b):
                roots[0] += 1
                act.wait_ge(var_ready, roots[0])
                nc.scalar.activation(std[:, b:b + 1], mv[:, b, 1:2], ACT.Sqrt, bias=eps[:, 0:1]).then_inc(std_ready, 1)

            def relu(l, b):
                act.wait_ge(norm_ready, l * NB + b + 1)
                return nc.scalar.activation(H[:, b, :], H[:, b, :], ACT.Relu)

            def high_part(b):
                act.wait_ge(act_step, b + 1)
                if b >= PARTS:
                    act.wait_ge(parts_out[b % PARTS], 16)
                nc.scalar.activation(parts[:, b % PARTS, 0, :], H[:, b, :], ACT.Copy, scale=SPLIT
                                     ).then_inc(relu_ready, 1)

            def copy_transposed(use, b):
                n = act_at[use]
                act.wait_ge(act_ready, n + 1)
                nc.scalar.copy(HT[:, b, :, 0:rows[b]],
                               act_ps[n % 2][:, :].rearrange("p (k n) -> p k n", k=KD)[:, :, 0:rows[b]]
                               ).then_inc(act_free, 1)

            def take_alpha(b):
                n = act_at[("a0", b)]
                act.wait_ge(act_ready, n + 1)
                nc.scalar.copy(X[0:rows[b], b, :], act_ps[n % 2][0:rows[b], :]).then_inc(act_free, 1)

            def copy_counts(l):
                with act.Fori(0, STEPS) as i:
                    for h in range(2):
                        act.wait_ge(slot_free[RING - 1], i * 2 + (l * HALVES + h + 2))
                        nc.scalar.copy(tile_counts[:, bass.ds(i * STEP + h * RING, RING)], act_ps[h][:, 0:RING]
                                       ).then_inc(counts_free, 1)

            for b in range(NB):
                square_root(b)
            for b in range(NB):
                relu(0, b).then_inc(act_step, 1)
                high_part(b)
                if b:
                    copy_transposed(("t0", b - 1), b - 1)
                if 2 <= b < 2 + EARLY:
                    take_alpha(b - 2)
            copy_transposed(("t0", NB - 1), NB - 1)
            for b in range(NB - 2, NB):
                if b < EARLY:
                    take_alpha(b)
            for b in range(EARLY, NB):
                take_alpha(b)
            copy_counts(0)
            for b in range(NB):
                square_root(b)
                if b:
                    relu(1, b - 1).then_inc(relu_ready, 1)
            relu(1, NB - 1).then_inc(relu_ready, 1)
            for b in range(NB):
                copy_transposed(("t1", b), b)
            copy_counts(1)
            first = node_groups[0]
            for b in first:
                square_root(b)
            for b in first:
                copy_transposed(("tx", b), b)
            for b in range(len(first), NB):
                square_root(b)
            act.wait_ge(rows_in, 16 * ROWS)
            act.wait_ge(acc_used, 1)
            for g, blocks in enumerate(node_groups):
                if g:
                    for b in blocks:
                        copy_transposed(("tx", b), b)
                for f in range(KF):
                    n = act_at[("w1", g, f)]
                    act.wait_ge(act_ready, n + 1)
                    at = 0
                    for b, nb, r in spans(blocks):
                        ins = nc.scalar.activation(gelu_out(f, slice(b, b + nb))[:, :, 0:r],
                                                   act_ps[n % 2][:, at:at + nb * r].rearrange("p (b n) -> p b n", b=nb),
                                                   ACT.Gelu, bias=b1_sb[:, f:f + 1])
                        at += nb * r
                    ins.then_inc(act_free, 1)
            for b in range(NB):
                square_root(b)

        @block.vector
        def _(dve):
            steps, norms = [0], [0]

            def mark(ins):
                ins.then_inc(dve_step, 1)
                steps[0] += 1

            def done(ins):
                mark(ins)
                dve.wait_ge(dve_step, steps[0])

            def moments(of, b):
                done(nc.vector.bn_stats(stats[:, b, :], of[:, b, :]))
                nc.vector.bn_aggr(mv[:, b, :], stats[:, b, :]).then_inc(var_ready, 1)

            def normalise(of, b):
                norms[0] += 1
                dve.wait_ge(std_ready, norms[0])
                done(nc.vector.reciprocal(rstd[:, b:b + 1], std[:, b:b + 1]))
                return nc.vector.tensor_scalar(H[:, b, :], of[:, b, :], mv[:, b, 0:1], rstd[:, b:b + 1],
                                               ALU.subtract, ALU.mult)

            def low_part(b):
                dve.wait_ge(relu_ready, b + 1)
                nc.vector.scalar_tensor_tensor(out=parts[:, b % PARTS, 1, :], in0=H[:, b, :], scalar=SPLIT,
                                               in1=parts[:, b % PARTS, 0, :], op0=ALU.mult, op1=ALU.subtract
                                               ).then_inc(low_ready, 1)

            def layer_norm_0():
                for b in range(NB):
                    dve.wait_ge(x_in[b], 16)
                    moments(X, b)
                for b in range(NB):
                    normalise(X, b).then_inc(norm_ready, 1)
                    if b >= 2:
                        low_part(b - 2)
                for b in (NB - 2, NB - 1):
                    low_part(b)

            def rank_counts(l):
                seg, other = edges[:, l, :], edges[:, 1 - l, :]
                done(nc.vector.tensor_scalar(int_a[:, :], seg, 7, None, ALU.logical_shift_right))
                done(nc.vector.tensor_copy(edge_f[:, :], int_a[:, :]))
                mark(nc.vector.tensor_scalar(int_b[:, :], seg, P - 1, None, ALU.bitwise_and))
                mark(nc.vector.tensor_scalar(edge_data[:, 2, 0:EC], other, 1.0, None, ALU.add))
                done(nc.vector.tensor_tensor(mask, edge_f[:, :].unsqueeze(1).to_broadcast([EP, NB, EC]),
                                             iota_key[:, :].unsqueeze(2).to_broadcast([EP, NB, EC]), ALU.is_equal))
                done(nc.vector.tensor_scalar(edge_f[:, :], int_b[:, :], 1.0, None, ALU.add))
                mark(nc.vector.scalar_tensor_tensor(out=edge_data[:, 3, 0:EC], in0=edges[:, 2, :],
                                                    scalar=float(l << TYPE_AT), in1=edge_f[:, :], op0=ALU.mult,
                                                    op1=ALU.add))
                done(nc.vector.tensor_tensor_scan(seen2, ones32[0:EP, 0:1].to_broadcast([EP, NB * EC]), mask2, 0.0,
                                                  ALU.mult, ALU.add))
                done(nc.vector.tensor_copy(last[:, :], seen[:, :, EC - 1]))
                mark(nc.vector.tensor_copy(counts16[:, 0:1], last[:, 0:1]))
                nc.vector.tensor_tensor(counts16[:, 1:NB], last[:, 1:NB], last[:, 0:NB - 1], ALU.subtract).then_inc(
                    small_free, 1)

            def rank_places(l):
                dve.wait_ge(small_ready, 2 * l + 1)
                below, total = small_ps[0:EP, 0:NB], small_ps[:, NB:2 * NB]
                done(nc.vector.tensor_scalar(total_i[:, :], total, float(P - 1), None, ALU.add))
                done(nc.vector.tensor_scalar(total_i[:, :], total_i[:, :], 7, None, ALU.logical_shift_right))
                done(nc.vector.tensor_copy(tiles_of[:, 0, :], total_i[:, :]))
                done(nc.vector.tensor_tensor_scan(tiles_of[:, 1, :], ones32[:, 0:1].to_broadcast([P, NB]),
                                                  tiles_of[:, 0, :], 0.0, ALU.mult, ALU.add))
                done(nc.vector.tensor_tensor(tiles_of[:, 2, :], tiles_of[:, 1, :], tiles_of[:, 0, :], ALU.subtract))
                for c in range(2):
                    for n, m in ((0, 1), (1, 2)):
                        mark(nc.vector.tensor_scalar(reached[:, n, c, :], tiles_of[:, m, :], index_p[:, c:c + 1], None,
                                                     ALU.is_le))
                dve.wait_ge(dve_step, steps[0])
                mark(nc.vector.tensor_tensor(tile_key[:, l, :, :], reached[:, 1, :, :], reached[:, 0, :, :],
                                             ALU.subtract))
                done(nc.vector.tensor_reduce(key_col[:, :], reached[:, 0, :, :], AX.X, ALU.add))
                nc.vector.tensor_scalar(key_col[:, :], key_col[:, :], float(NB - 1), None, ALU.min).then_inc(small_free, 1)
                done(nc.vector.scalar_tensor_tensor(out=place0[:, :], in0=tiles_of[0:EP, 2, :], scalar=float(P),
                                                    in1=below, op0=ALU.mult, op1=ALU.add))
                done(nc.vector.tensor_scalar(place0[:, :], place0[:, :], -1.0, None, ALU.add))
                done(nc.vector.tensor_tensor(place0[:, 1:NB], place0[:, 1:NB], last[:, 0:NB - 1], ALU.subtract))
                nc.vector.sem_inc(small_free, 1)
                done(nc.vector.tensor_tensor(place, seen, place0[:, :].unsqueeze(2).to_broadcast([EP, NB, EC]), ALU.add))
                done(nc.vector.tensor_tensor(place, place, mask, ALU.mult))
                done(nc.vector.tensor_reduce(edge_f[:, :], place.rearrange("p k j -> p j k"), AX.X, ALU.add))
                done(nc.vector.tensor_copy(int_a[:, :], edge_f[:, :]))
                mark(nc.vector.tensor_scalar(int_b[:, :], int_a[:, :], 7, None, ALU.logical_shift_right))
                done(nc.vector.tensor_scalar(int_a[:, :], int_a[:, :], P - 1, None, ALU.bitwise_and))
                mark(nc.vector.tensor_copy(edge_data[:, 0, 0:EC], int_a[:, :]))
                done(nc.vector.tensor_copy(edge_data[:, 1, 0:EC], int_b[:, :]))
                dve.wait_ge(small_ready, 2 * l + 2)
                done(nc.vector.tensor_copy(key_row[0:1, l, :], small_ps[0:1, 0:2 * P]))

            def permute_ops(l, i, h):
                def data(n, width):
                    return edge_data[:, n, bass.ds(i * STEP + h * RING, RING)].unsqueeze(1).to_broadcast(
                        [EP, width, RING])

                def by_slot():
                    dve.wait_ge(perm_used, i * 2 + (l * HALVES + h + 1))
                    nc.vector.tensor_tensor(slot_onehot[:, h], iota_rep[0:EP, 0:P, :], data(0, P), ALU.is_equal
                                            ).then_inc(slot_made, 1)

                def times_row():
                    dve.wait_ge(slot_made, i * 2 + (l * HALVES + h + 1))
                    nc.vector.tensor_tensor(row_onehot[:, h], slot_onehot[:, h], data(2, P), ALU.mult)

                def times_segment():
                    nc.vector.tensor_tensor(seg_onehot[:, h], slot_onehot[:, h], data(3, P), ALU.mult)

                def by_tile():
                    nc.vector.tensor_tensor(tile_onehot[:, h], iota_rep[0:EP, :, :], data(1, T), ALU.is_equal
                                            ).then_inc(perm_ready, 1)

                return [by_slot, times_row, times_segment, by_tile]

            def lists(l):
                dve.wait_ge(perm_done, l + 1)
                row, seg = gather_f[:, 0, :], gather_f[:, 1, :]
                mark(nc.vector.tensor_scalar(row, perm_ps[:, 0:T], 0.0, 4096.0, ALU.is_equal, ALU.mult))
                done(nc.vector.tensor_copy(payload_i[:, 0, :], perm_ps[:, T:2 * T]))
                mark(nc.vector.tensor_scalar(payload_i[:, 1, :], payload_i[:, 0, :], TYPE_AT, None,
                                             ALU.logical_shift_right))
                done(nc.vector.tensor_scalar(payload_i[:, 0, :], payload_i[:, 0, :], 2 ** TYPE_AT - 1, None,
                                             ALU.bitwise_and))
                mark(nc.vector.tensor_scalar(segrow[:, 0:T], payload_i[:, 0, :], -1.0, None, ALU.add))
                done(nc.vector.scalar_tensor_tensor(out=row, in0=perm_ps[:, 0:T], scalar=-1.0, in1=row, op0=ALU.add,
                                                    op1=ALU.add))
                done(nc.vector.scalar_tensor_tensor(out=gidx[:, 0:T], in0=row, scalar=float((1, R)[l]),
                                                    in1=payload_i[:, 1, :], op0=ALU.mult, op1=ALU.add))
                nc.vector.sem_inc(lists_ready, 1)

            def prepare(l, q, at, buf):
                if not (isinstance(q, int) and q == 0):
                    dve.wait_ge(slot_free[RING - 1], q)
                nc.vector.tensor_copy(gidx_now[:, buf, :], gidx[:, bass.ds(at, RING)]).then_inc(stage_ready, 1)
                nc.vector.tensor_tensor((segment_onehot16, segment_onehot)[l][:, buf],
                                        iota_col[:, :].unsqueeze(1).to_broadcast([P, RING, P]),
                                        segrow[:, bass.ds(at, RING)].unsqueeze(2).to_broadcast([P, RING, P]),
                                        ALU.is_equal).then_inc(onehot_ready, 1)

            regs = [dve.alloc_register(f"key{u}") for u in range(STEP)]

            def gather(l):
                prepare(l, l * (HALVES + 1), 0, 0)
                with dve.Fori(0, STEPS) as i:
                    dve.load(regs, key_row[0:1, l, bass.ds(i * STEP, STEP)])
                    keys = [dve.snap(r, min_val=0, max_val=NB - 1) for r in regs]
                    for h in range(2):
                        prepare(l, i * 2 + (l * HALVES + h + 1), i * STEP + (h + 1) * RING, 1 - h)
                        extra = permute_ops(1, i, 0) + permute_ops(1, i, 1) if (l, h) == (0, 0) else []
                        for s in range(RING):
                            u = h * RING + s
                            if extra:
                                extra.pop(0)()
                            n = i * STEP + (GBASE[l] + u + 1)
                            dve.wait_ge(ring_ready, n)
                            dve.wait_ge(ring_free, n + 3)
                            a = ACC[:, bass.ds(keys[u], 1), :]
                            nc.vector.tensor_tensor(a, a, ring[(GBASE[l] + u) % 4][:, :].unsqueeze(1), ALU.add
                                                    ).then_inc(ring_free, 1)

            def counts(l):
                dve.wait_ge(small_ready, 2 * l + 5)
                mark(nc.vector.tensor_copy(tile_counts_t[:, 0, :], small_ps[:, 0:P]))
                nc.vector.tensor_copy(tile_counts_t[0:T - P, 1, :], small_ps[0:T - P, P:2 * P]).then_inc(small_free, 1)
                dve.wait_ge(small_ready, 2 * l + 6)
                if l == 0:
                    r = rows[NB - 1]
                    done(nc.vector.memset(inv[:, 0, NB - 1:NB], 0.0))
                    mark(nc.vector.reciprocal(inv[:, 0, 0:NB - 1], small_ps[:, 0:NB - 1]))
                    done(nc.vector.reciprocal(inv[0:r, 0, NB - 1:NB], small_ps[0:r, NB - 1:NB]))
                    done(nc.vector.tensor_scalar(inv[:, 0, :], inv[:, 0, :], 1.0 / SPLIT, None, ALU.mult))
                else:
                    done(nc.vector.tensor_scalar(inv[:, 1, :], small_ps[:, 0:NB], 1.0, None, ALU.max))
                    done(nc.vector.reciprocal(inv[:, 1, :], inv[:, 1, :]))

            dve.wait_ge(consts, 2)
            mark(nc.vector.tensor_scalar(ident[:, :], iota_col[:, :], index_p[:, 0:1], None, ALU.is_equal))
            done(nc.vector.tensor_scalar(upper16[:, :], iota_col[:, :], index_p[:, 0:1], None, ALU.is_gt))
            nc.vector.sem_inc(ring_free, 4)
            nc.vector.sem_inc(consts, 1)

            dve.wait_ge(edges_in, 96)
            layer_norm_0()
            rank_counts(0)
            rank_places(0)
            dve.wait_ge(consts, 4)
            with dve.Fori(0, STEPS) as i:
                for h in range(2):
                    for op in permute_ops(0, i, h):
                        op()
            lists(0)
            rank_counts(1)
            rank_places(1)
            dve.wait_ge(acc_clear, 1)
            gather(0)
            lists(1)
            counts(0)
            for b in range(NB):
                r = rows[b]
                dve.wait_ge(ring_ready, B0 + b + 1)
                nc.vector.scalar_tensor_tensor(out=X[0:r, b, :], in0=ring[(B0 + b) % 4][0:r, :],
                                               scalar=inv[0:r, 0, b:b + 1], in1=X[0:r, b, :], op0=ALU.mult, op1=ALU.add
                                               ).then_inc(ring_free, 1)
                dve.wait_ge(ring_free, 4 + B0 + b + 1)
                moments(X, b)
                if b:
                    normalise(X, b - 1).then_inc(norm_ready, 1)
            normalise(X, NB - 1).then_inc(norm_ready, 1)
            dve.wait_ge(rows_in, 16 * ROWS)
            for n in range(NB * R):
                slot = n // 2
                if n % 2 == 0 and slot >= OUTS:
                    dve.wait_ge(messages_out[slot % OUTS], 16 * uses_of(slot % OUTS, OUTS, slot))
                dve.wait_ge(ring_ready, M1 + n + 1)
                ins = nc.vector.tensor_tensor(out_slots[:, slot % OUTS, n % 2, :], ring[(M1 + n) % 4][:, :],
                                              relb_sb[:, n % R, :], ALU.add)
                ins.then_inc(ring_free, 1)
                if n % 2:
                    dve.wait_ge(ring_free, 4 + M1 + n + 1)
                    nc.vector.sem_inc(message_ready, 1)
            for b in range(NB):
                r = rows[b]
                dve.wait_ge(ring_ready, S1 + b + 1)
                nc.vector.tensor_tensor(H[0:r, b, :], H[0:r, b, :], ring[(S1 + b) % 4][0:r, :], ALU.add
                                        ).then_inc(ring_free, 1)
            dve.wait_ge(acc_clear, 2)
            gather(1)
            counts(1)
            for b in range(NB):
                ins = nc.vector.scalar_tensor_tensor(out=H[:, b, :], in0=ACC[:, b, :], scalar=inv[:, 1, b:b + 1],
                                                     in1=H[:, b, :], op0=ALU.mult, op1=ALU.add)
                mark(ins)
            dve.wait_ge(dve_step, steps[0])
            nc.vector.sem_inc(acc_used, 1)

            def weighted_norm(b, w):
                done(normalise(H, b))
                done(nc.vector.tensor_tensor(H[:, b, :], H[:, b, :], w[:, 0, :], ALU.mult))
                return nc.vector.tensor_tensor(H[:, b, :], H[:, b, :], w[:, 1, :], ALU.add)

            for b in range(NB):
                moments(H, b)
                if b:
                    weighted_norm(b - 1, ln1).then_inc(x1_ready, 1)
            weighted_norm(NB - 1, ln1).then_inc(x1_ready, 1)
            for b in range(NB):
                dve.wait_ge(act_ready, act_at[("tx", b)] + 1)
                mark(nc.vector.tensor_tensor(H[:, b, :], H[:, b, :], b2_sb[:, :], ALU.add))
            dve.wait_ge(dve_step, steps[0])

            def output(b):
                r = rows[b]
                done(weighted_norm(b, ln2))
                nc.vector.tensor_tensor(X[0:r, b, :], X[0:r, b, :], H[0:r, b, :], ALU.add).then_inc(y_ready, 1)

            for b in range(NB):
                r = rows[b]
                dve.wait_ge(ring_ready, F1 + b + 1)
                nc.vector.tensor_tensor(H[0:r, b, :], H[0:r, b, :], ring[(F1 + b) % 4][0:r, :], ALU.add
                                        ).then_inc(ring_free, 1)
                dve.wait_ge(ring_free, 4 + F1 + b + 1)
                moments(H, b)
                if b:
                    output(b - 1)
            output(NB - 1)

        @block.tensor
        def _(pe):
            pe.wait_ge(consts, 4)

            def mm(*a, **k):
                return nc.tensor.matmul(*a, **k)

            def act_bank(n):
                if n >= 2:
                    pe.wait_ge(act_free, n - 1)
                return act_ps[n % 2]

            def transposes(use, b, ready, value):
                n = act_at[use]
                pe.wait_ge(ready, value)
                bank = act_bank(n)
                for k in range(KD):
                    ins = nc.tensor.transpose(bank[:, k * P:k * P + rows[b]], H[0:rows[b], b, k * P:(k + 1) * P],
                                              ident[0:rows[b], 0:rows[b]])
                ins.then_inc(act_ready, 1)

            def products(bank, b, terms):
                for m, (left, right) in enumerate(terms):
                    ins = mm(bank[0:rows[b], :], left, right, start=(m == 0), stop=(m == len(terms) - 1))
                return ins

            def node_product(n, b, terms):
                pe.wait_ge(ring_free, n + 1)
                products(ring[n % 4], b, terms).then_inc(ring_ready, 1)

            def of_block(b, w):
                return [(HT[:, b, k, 0:rows[b]], w[:, k, :]) for k in range(KD)]

            def row_bias(b, n):
                return [(ones32[0:1, 0:rows[b]], bias_rows[0:1, n, :])]

            def alpha(b):
                n = act_at[("a0", b)]
                pe.wait_ge(act_free, act_at[("t0", b)] + 1)
                bank = act_bank(n)
                products(bank, b, of_block(b, wa) + row_bias(b, 0) + [(ident[0:P, 0:rows[b]], X[:, b, :])]
                         ).then_inc(act_ready, 1)

            def rank_counts(l):
                pe.wait_ge(small_free, 3 * l + 1)
                mm(small_ps[0:EP, 0:NB], upper16[0:EP, 0:EP], counts16[:, :], start=True, stop=True)
                mm(small_ps[:, NB:2 * NB], ones16[0:EP, :], counts16[:, :], start=True, stop=True
                   ).then_inc(small_ready, 1)

            def key_rows(l):
                pe.wait_ge(small_free, 3 * l + 3)
                for c in range(2):
                    ins = mm(small_ps[0:1, c * P:(c + 1) * P], key_col[:, c:c + 1], ident[:, :], start=True, stop=True)
                ins.then_inc(small_ready, 1)

            def permute_zeros(l, first):
                if first and l:
                    pe.wait_ge(lists_ready, l)
                return mm(perm_ps[:, 0:2 * T], zeros16[0:EP, 0:P], zeros16[0:EP, :], start=first, stop=not first)

            def permute_column(l, i, h, c):
                if c == 0:
                    pe.wait_ge(perm_ready, i * 2 + (l * HALVES + h + 1))
                mm(perm_ps[:, 0:T], row_onehot[:, h, :, c], tile_onehot[:, h, :, c], start=False, stop=False)
                ins = mm(perm_ps[:, T:2 * T], seg_onehot[:, h, :, c], tile_onehot[:, h, :, c], start=False, stop=False)
                if c == RING - 1:
                    ins.then_inc(perm_used, 1)

            def gather(l):
                with pe.Fori(0, STEPS) as i:
                    half = [pe.snap(i * 2 + (l * HALVES + h + 1)) for h in range(2)]
                    arrived = [pe.snap(i * 32 + 16 * (l * HALVES + h + 1)) for h in range(2)]
                    for h in range(2):
                        pe.wait_ge(onehot_ready, half[h] + l)
                        pe.wait_ge(counts_free, half[h])
                        for s in range(RING):
                            u = h * RING + s
                            pe.wait_ge(tile_in[s], arrived[h])
                            pe.wait_ge(ring_free, i * STEP + (GBASE[l] + u + 1))
                            bank = ring[(GBASE[l] + u) % 4]
                            if l == 0:
                                onehot = segment_onehot16[:, h, s, :]
                                for k in range(KD):
                                    for part in range(2):
                                        ins = mm(bank[:, k * P:(k + 1) * P],
                                                 gathered16[:, s, part * D + k * P:part * D + (k + 1) * P], onehot,
                                                 start=(part == 0), stop=(part == 1))
                            else:
                                onehot = segment_onehot[:, h, s, :]
                                ins = mm(bank[:, :], onehot, gathered[:, s, :], start=True, stop=True)
                            ins.then_inc(ring_ready, 1)
                            mm(act_ps[h][:, s:s + 1], onehot, (ones16, ones32)[l][:, 0:1], start=True, stop=True
                               ).then_inc(slot_free[s], 1)
                            if l == 0 and u >= RING:
                                for c in range(2 * (u - RING), 2 * (u - RING) + 2):
                                    permute_column(1, i, c // RING, c % RING)

            def counts(l):
                pe.wait_ge(counts_free, 2 + HALVES * (l + 1))
                nc.tensor.transpose(small_ps[:, 0:P], tile_counts[:, 0:P], ident[:, :])
                nc.tensor.transpose(small_ps[0:T - P, P:2 * P], tile_counts[:, P:T], ident[:, :]).then_inc(small_ready, 1)
                pe.wait_ge(small_free, l + 7)
                for c, t in ((0, P), (1, T - P)):
                    ins = mm(small_ps[:, 0:NB], tile_counts_t[0:t, c, :], tile_key[0:t, l, c, :], start=(c == 0),
                             stop=(c == 1))
                ins.then_inc(small_ready, 1)

            def t0(b):
                transposes(("t0", b), b, relu_ready, b + 1)

            t0(0)
            for b in range(NB):
                if b + 1 < NB:
                    t0(b + 1)
                if b == 0:
                    pe.wait_ge(wa_in, 16)
                    pe.wait_ge(rows_in, 16 * ROWS)
                if b < EARLY:
                    alpha(b)
            rank_counts(0)
            key_rows(0)
            pe.sem_inc(perm_used, 2)
            pe.sem_inc(counts_free, 2)
            permute_zeros(0, True)
            with pe.Fori(0, STEPS) as i:
                for h in range(2):
                    for c in range(RING):
                        permute_column(0, i, h, c)
            permute_zeros(0, False).then_inc(perm_done, 1)
            for b in range(EARLY, NB - 2):
                alpha(b)
            rank_counts(1)
            alpha(NB - 2)
            key_rows(1)
            alpha(NB - 1)
            permute_zeros(1, True)
            pe.wait_ge(act_free, act_at[("a0", NB - 1)] + 1)
            gather(0)
            permute_zeros(1, False).then_inc(perm_done, 1)
            counts(0)
            pe.wait_ge(wb_in, 16)
            pe.wait_ge(ring_free, 4 + B0)
            for b in range(NB):
                node_product(B0 + b, b, [(ACC[:, b, k * P:k * P + rows[b]], wb[:, k, :]) for k in range(KD)])
            transposes(("t1", 0), 0, relu_ready, NB + 1)
            pe.wait_ge(relw_in, 16)
            for b in range(NB):
                if b + 1 < NB:
                    transposes(("t1", b + 1), b + 1, relu_ready, NB + b + 2)
                pe.wait_ge(act_free, act_at[("t1", b)] + 1)
                for r in range(R):
                    node_product(M1 + b * R + r, b, of_block(b, relw_sb[:, r]))
            pe.wait_ge(wa_in, 32)
            for b in range(NB):
                node_product(S1 + b, b, of_block(b, wa) + row_bias(b, 1))
            gather(1)
            counts(1)
            pe.wait_ge(w1_in, 16)
            for g, blocks in enumerate(node_groups):
                for b in blocks:
                    transposes(("tx", b), b, x1_ready, b + 1)
                pe.wait_ge(act_free, act_at[("tx", blocks[-1])] + 1)
                for f in range(KF):
                    n = act_at[("w1", g, f)]
                    bank = act_bank(n)
                    at = 0
                    for b, nb, r in spans(blocks):
                        for k in range(KD):
                            ins = mm(bank[:, at:at + nb * r], w1_sb[:, k, f::KF], HT[:, b:b + nb, k, 0:r],
                                     start=(k == 0), stop=(k == KD - 1))
                        at += nb * r
                    ins.then_inc(act_ready, 1)
            pe.wait_ge(w2_in, 16)
            for g, blocks in enumerate(node_groups):
                pe.wait_ge(act_free, act_at[("w1", g, KF - 1)] + 1)
                for b in blocks:
                    node_product(F1 + b, b, [(gelu_out(f, b)[:, 0:rows[b]], w2_sb[:, f, :]) for f in range(KF)])


_INS = ['x', 'src', 'dst', 'edge_type_4', 'L0_gnn_wc', 'L0_gnn_wn', 'L0_gnn_bias', 'L1_gnn_self_W', 'L1_gnn_self_b',
        'L1_gnn_rel_W', 'L1_gnn_rel_b', 'L1_gnn_ln1_w', 'L1_gnn_ln1_b', 'L1_gnn_W1', 'L1_gnn_b1', 'L1_gnn_W2',
        'L1_gnn_b2', 'L1_gnn_ln2_w', 'L1_gnn_ln2_b']


def kernel(**inputs):
    import numpy as _np
    import concourse.bacc as _bacc
    from concourse import mybir as _mybir
    from concourse.bass_utils import run_bass_kernel_spmd as _run

    nc = _bacc.Bacc("TRN2", target_bir_lowering=False, num_devices=1)
    arrays, args = {}, []
    for name in _INS:
        a = _np.ascontiguousarray(inputs[name])
        arrays[f"in_{name}_dram"] = a
        args.append(nc.dram_tensor(f"in_{name}_dram", a.shape, _mybir.dt.from_np(a.dtype), kind="ExternalInput").ap())
    shape = inputs['x'].shape
    args.append(nc.dram_tensor("out_0_dram", shape, _mybir.dt.float32, kind="ExternalOutput").ap())
    build_gnn(nc, *args)
    r = _run(nc, [arrays], core_ids=[0])
    return r.results[0]["out_0_dram"]
```

```python
import concourse.bass as bass
from concourse import mybir
from contextlib import ExitStack


def build_gnn(nc, x, src, dst, etype, wc, wn, bias0, self_w, self_b, rel_w, rel_b, ln1_w, ln1_b, w1, b1, w2, b2,
              ln2_w, ln2_b, out):
    fp32, fp32r, fp16, i32 = mybir.dt.float32, mybir.dt.float32r, mybir.dt.float16, mybir.dt.int32
    ALU, ACT, AX = mybir.AluOpType, mybir.ActivationFunctionType, mybir.AxisListType

    N, D = x.shape
    E = src.shape[0]
    R = rel_w.shape[0]
    F = w1.shape[1]
    P = 128
    EPS = 1e-5
    SPLIT = 2048.0
    TYPE_AT = 8
    BY_SCALAR = [6, 8]
    NB = -(-N // P)
    KD = D // P
    KF = F // P
    rows = [min(P, N - b * P) for b in range(NB)]
    EP = 125
    EC = E // EP
    assert EP * EC == E and N < 2048 and (R - 1) * 2 ** TYPE_AT + P < 2048

    RING = 8
    STEP = 2 * RING
    STEPS = -(-((E + NB * (P - 1)) // P) // STEP)
    T = STEP * STEPS
    HALVES = 2 * STEPS
    assert T >= EC and 2 * T + NB <= 512

    G0 = 0
    B0 = G0 + T
    M1 = B0 + NB
    S1 = M1 + R * NB
    G1 = S1 + NB
    F1 = G1 + T
    GBASE = [G0, G1]

    act_uses = [(use, b) for use in ("t0", "t1") for b in range(NB)]
    act_at = {u: n for n, u in enumerate(act_uses)}

    GROUP = 3
    node_groups = [list(range(2))] + [list(range(g, min(g + GROUP, NB))) for g in range(2, NB, GROUP)]
    group_of = {b: g for g, blocks in enumerate(node_groups) for b in blocks}
    ffn_order = []

    def transpose_next(ahead=2):
        b = sum(part == "tx" for part, _ in ffn_order)
        while sum(part == "x1" for part, _ in ffn_order) < min(b + ahead, NB) + 1:
            ffn_order.append(("x1", sum(part == "x1" for part, _ in ffn_order)))
        ffn_order.append(("tx", b))

    for _ in node_groups[0]:
        transpose_next(ahead=1)
    for g, blocks in enumerate(node_groups):
        coming = len(node_groups[g + 1]) if g + 1 < len(node_groups) else 0
        for f in range(KF):
            ffn_order.append(("w1", g * KF + f))
            if f % 2 and coming:
                transpose_next()
                coming -= 1
        ffn_order += [("w2", b) for b in blocks]

    h0_table = nc.dram_tensor("h0_table", [N, 2 * D], fp16, kind="Internal").ap()
    message_table = nc.dram_tensor("message_table", [N, R * D], fp32, kind="Internal").ap()
    gather_from = [h0_table, message_table.rearrange("n (r d) -> (n r) d", r=R)]
    last_row = [N - 1, N * R - 1]

    ctx = ExitStack()
    with ctx:
        def sb(name, shape, dt=fp32):
            return ctx.enter_context(nc.sbuf_tensor(name, shape, dt))

        def ps(name, shape, dt=fp32):
            return ctx.enter_context(nc.psum_tensor(name, shape, dt))

        def sem(name):
            return ctx.enter_context(nc.semaphore(name))

        assert STEPS == NB + 1
        X = sb("X", [P, NB, D])
        H = sb("H", [P, STEPS, D])
        h0_block = sb("h0_block", [P, KD, P])

        zone_words = []

        def overlay(*tensors):
            with ExitStack() as stack:
                handles = [stack.enter_context(nc.sbuf_tensor(name, shape, dt)) for name, shape, dt in tensors]
            words = 0
            for _, shape, dt in tensors:
                n = 1
                for size in shape[1:]:
                    n *= size
                words += n // 2 if dt == fp16 else n
            zone_words.append(words)
            return handles

        TILES = RING * D + 2 * RING * P
        HT, ACC, tiles, region, wa, wb, relb_sb, out_slots, iota_rep, edges = overlay(
            ("HT", [P, STEPS, KD, P], fp32),
            ("ACC", [P, NB, D], fp32),
            ("tiles", [P, TILES], fp32),
            ("region", [P, 4 * KD * D], fp32),
            ("wa", [P, KD, D], fp32),
            ("wb", [P, KD, D], fp32),
            ("relb_sb", [P, R, D], fp32),
            ("out_slots", [P, 6, D], fp32),
            ("iota_rep", [P, T, RING], fp16),
            ("edges", [P, 3, EC], i32))
        PARTS = OUTS = 6
        parts = out_slots[:, :, :].rearrange("p s d -> p (s d)").bitcast(fp16).rearrange(
            "p (s t d) -> p s t d", s=PARTS, t=2)

        gathered = tiles[:, 0:RING * D].rearrange("p (s n) -> p s n", s=RING)
        gathered16 = tiles[:, 0:RING * D].bitcast(fp16).rearrange("p (s n) -> p s n", s=RING)
        segment_onehot = tiles[:, RING * D:].rearrange("p (h s n) -> p h s n", h=2, s=RING)
        segment_onehot16 = tiles[:, RING * D:RING * D + RING * P].bitcast(fp16).rearrange(
            "p (h n s) -> p h n s", h=2, s=RING)
        cut = [0]

        def scratch(words):
            cut[0] += words
            return region[0:EP, cut[0] - words:cut[0]]

        mask2 = scratch(NB * T // 2).bitcast(fp16)
        seen2 = scratch(NB * T // 2).bitcast(fp16)
        mask = mask2.rearrange("p (k j) -> p k j", k=NB)
        seen = seen2.rearrange("p (k j) -> p k j", k=NB)
        place2 = scratch(NB * EC)
        place = place2.rearrange("p (k j) -> p k j", k=NB)
        count_onehot = place2[:, 0:P * STEP // 2].bitcast(fp16).rearrange("p (h n j) -> p h n j", h=2, j=RING)
        slot_onehot, row_onehot, seg_onehot = (
            scratch(P * STEP // 2).bitcast(fp16).rearrange("p (h n j) -> p h n j", h=2, j=RING) for _ in range(3))
        tile_onehot = scratch(T * STEP // 2).bitcast(fp16).rearrange("p (h n j) -> p h n j", h=2, j=RING)
        assert cut[0] <= 4 * KD * D

        h1_high, h1_low, _, w_parts1, _, w_parts0, w_loaded = overlay(
            ("h1_high", [P, NB, KD, P], fp32r), ("h1_low", [P, NB, KD, P], fp32r),
            ("unused0", [P, (STEPS - NB) * D], fp32),
            ("w_parts1", [P, 2, KD, D], fp32r), ("unused1", [P, TILES - 2 * KD * D], fp32),
            ("w_parts0", [P, 2, KD, D], fp32r), ("w_loaded", [P, 2, KD, D], fp32))
        w_parts = [w_parts0, w_parts1]

        FFN_WORDS = KD * F + KF * D
        PIECE = -(-FFN_WORDS // (STEPS * 256)) * 256
        HELD = PIECE * STEPS
        GN = GROUP * P
        SPARE = (STEPS - NB) * D - GN
        x1_high, gelu0, _, x1_low, gelu_high, gelu_low, ffn_loaded, ffn_high, gelu1, _, ln2 = overlay(
            ("x1_high", [P, NB, KD, P], fp32r), ("gelu0", [P, GN], fp32), ("unused2", [P, SPARE], fp32),
            ("x1_low", [P, NB, KD, P], fp32r),
            ("gelu_high", [P, KF, GN], fp32r), ("gelu_low", [P, KF, GN], fp32r),
            ("ffn_loaded", [P, HELD], fp32), ("ffn_high", [P, HELD], fp32r),
            ("gelu1", [P, GN], fp32), ("unused3", [P, SPARE], fp32),
            ("ln2", [P, 2, D], fp32))
        gelu = [gelu0, gelu1]
        _, ffn_low = overlay(("unused4", [P, STEPS * D + NB * D + TILES], fp32), ("ffn_low", [P, HELD], fp32r))
        assert 2 * KF * GN == TILES
        w1_parts = [w[:, 0:KD * F].rearrange("p (k n) -> p k n", k=KD) for w in (ffn_high, ffn_low)]
        w2_parts = [w[:, KD * F:FFN_WORDS].rearrange("p (k n) -> p k n", k=KF) for w in (ffn_high, ffn_low)]
        sb("zone", [P, max(zone_words)])
        ln1 = sb("ln1", [P, 2, D])
        bias_sb = sb("bias_sb", [P, D])
        b1_sb = sb("b1_sb", [P, KF])

        int_a = sb("int_a", [EP, EC], i32)
        int_b = sb("int_b", [EP, EC], i32)
        edge_f = sb("edge_f", [EP, EC])
        edge_block = sb("edge_block", [EP, T], fp16)
        mask_now = sb("mask_now", [EP, 2, NB, RING], fp16)
        edge_data = sb("edge_data", [EP, 4, T], fp16)
        row_f = sb("row_f", [EP, T])
        type_row = sb("type_row", [EP, T])
        last = sb("last", [EP, NB], fp16)
        counts16 = sb("counts16", [EP, NB], fp16)
        place0 = sb("place0", [EP, NB])
        total_i = sb("total_i", [P, NB], i32)
        tiles_of = sb("tiles_of", [P, 3, NB])
        reached = sb("reached", [P, 2, 2, NB])
        tile_key = sb("tile_key", [P, 2, 2, NB])
        key_col = sb("key_col", [P, 2])
        key_row = sb("key_row", [1, 2, 2 * P], i32)
        gidx = sb("gidx", [P, T + 2 * RING], i32)
        gather_f = sb("gather_f", [P, T])
        payload_i = sb("payload_i", [P, 2, T], i32)
        gidx_now = sb("gidx_now", [P, 2, RING], i32)
        segrow16 = sb("segrow16", [P, T + RING], fp16)
        segrow = sb("segrow", [P, T + RING])
        tile_counts = sb("tile_counts", [P, T])
        tile_counts_t = sb("tile_counts_t", [P, 2, P])
        inv = sb("inv", [P, 2, NB])
        stats = sb("stats", [P, NB, 6])
        mv = sb("mv", [P, NB, 2])
        var_eps = sb("var_eps", [P, NB])
        rstd = sb("rstd", [P, NB])

        iota_col = sb("iota_col", [P, P])
        index_p = sb("index_p", [P, 2])
        ident = sb("ident", [P, P])
        upper16 = sb("upper16", [P, P], fp16)
        ones16 = sb("ones16", [P, P], fp16)
        ones32 = sb("ones32", [P, P])
        minus_half = sb("minus_half", [P, 1])
        zeros16 = sb("zeros16", [P, 2 * T + NB], fp16)

        ring = [ps(f"ring{n}", [P, D]) for n in range(4)]
        perm_ps = ps("perm_ps", [P, 512])
        small_ps = ps("small_ps", [P, 512])
        act_ps = [ps(f"act_ps{n}", [P, 512]) for n in range(2)]
        x1_ps = [perm_ps, small_ps]

        edges_in = sem("edges_in")
        x_in = [sem(f"x_in{b}") for b in range(NB)]
        wa_in, wb_in, ln2_in = (sem(n) for n in ("wa_in", "wb_in", "ln2_in"))
        ffn_in = sem("ffn_in")
        ffn_high_made, ffn_low_made = sem("ffn_high_made"), sem("ffn_low_made")
        pad_clear = sem("pad_clear")
        x1_transposed = sem("x1_transposed")
        x1_high_made, x1_low_made = sem("x1_high_made"), sem("x1_low_made")
        mlp_ready, mlp_read = sem("mlp_ready"), sem("mlp_read")
        gelu_high_made, gelu_low_made = sem("gelu_high_made"), sem("gelu_low_made")
        w_loaded_in = [sem(f"w_loaded_in{s}") for s in range(2)]
        w_high, w_low = sem("w_high"), sem("w_low")
        h1_high_ready = sem("h1_high_ready")
        rows_in = sem("rows_in")
        bias_in = sem("bias_in")
        x_biased = sem("x_biased")
        self_biased = sem("self_biased")
        h0_staged = sem("h0_staged")
        alpha_done, alpha_taken = sem("alpha_done"), sem("alpha_taken")
        parts_out = [sem(f"parts_out{s}") for s in range(PARTS)]
        messages_out = [sem(f"messages_out{s}") for s in range(OUTS)]
        out_done = sem("out_done")
        pool_step, dve_step = sem("pool_step"), sem("dve_step")
        consts = sem("consts")
        ring_ready = sem("ring_ready")
        ring_free = sem("ring_free")
        act_ready, act_free = sem("act_ready"), sem("act_free")
        small_ready, small_free = sem("small_ready"), sem("small_free")
        perm_ready = sem("perm_ready")
        slot_made = sem("slot_made")
        times_type_row = sem("times_type_row")
        perm_used, perm_done = sem("perm_used"), sem("perm_done")
        lists_ready = sem("lists_ready")
        stage_ready = sem("stage_ready")
        STAGED = 3 + 2 * HALVES
        onehot_ready = sem("onehot_ready")
        tile_in = [sem(f"tile_in{s}") for s in range(RING)]
        slot_free = [sem(f"slot_free{s}") for s in range(RING)]
        counts_free = sem("counts_free")
        acc_clear = sem("acc_clear")
        half_added = sem("half_added")
        acc_used = sem("acc_used")
        var_ready, rstd_ready = sem("var_ready"), sem("rstd_ready")
        norm_ready = sem("norm_ready")
        relu_ready = sem("relu_ready")
        high_ready = sem("high_ready")
        low_ready = sem("low_ready")
        message_ready = sem("message_ready")
        x1_ready = sem("x1_ready")
        y_ready = sem("y_ready")

        block = ctx.enter_context(nc.Block())

        def uses_of(s, slots, upto):
            return len(range(s, upto, slots))

        ROWS = 1 + R + 2

        @block.sync
        def _(sp):
            def load_weights(m):
                w = rel_w[m] if m < R else self_w
                sp.dma_start(w_loaded[:, m % 2], w.rearrange("(k p) n -> p k n", p=P)).then_inc(w_loaded_in[m % 2], 16)

            for n, e in enumerate((src, dst, etype)):
                for lo, hi in ((0, 112), (112, EP)):
                    sp.dma_start(edges[lo:hi, n, :], e[lo * EC:hi * EC].rearrange("(p j) -> p j", j=EC)
                                 ).then_inc(edges_in, 16)
            sp.wait_ge(consts, 1)
            for b in range(NB):
                sp.dma_start(X[0:rows[b], b, :], x[b * P:b * P + rows[b], :]).then_inc(x_in[b], 16)
            sp.dma_start(wa[:, :, :], wc.rearrange("(k p) n -> p k n", p=P)).then_inc(wa_in, 16)
            sp.dma_start(bias_sb[:, :], bias0.partition_broadcast(P)).then_inc(bias_in, 16)
            sp.dma_start(b1_sb[:, :], b1.rearrange("(p k) -> p k", p=P)).then_inc(rows_in, 16)
            for r in range(R):
                sp.dma_start(relb_sb[:, r, :], rel_b[r, :].partition_broadcast(P)).then_inc(rows_in, 16)
            for n, v in enumerate((ln1_w, ln1_b)):
                sp.dma_start(ln1[:, n, :], v.partition_broadcast(P)).then_inc(rows_in, 16)
            sp.dma_start(wb[:, :, :], wn.rearrange("(k p) n -> p k n", p=P)).then_inc(wb_in, 16)
            for b in range(NB):
                sp.wait_ge(high_ready, b + 1)
                sp.wait_ge(low_ready, b + 1)
                sp.dma_start(h0_table[b * P:b * P + rows[b], :],
                             parts[0:rows[b], b % PARTS].rearrange("p t d -> p (t d)")
                             ).then_inc(parts_out[b % PARTS], 16)
            sp.wait_ge(x_biased, NB)
            sp.dma_start(bias_sb[:, :], self_b.partition_broadcast(P)).then_inc(bias_in, 16)
            sp.wait_ge(lists_ready, 2)
            load_weights(0)
            load_weights(1)
            for n in range(R * NB):
                m, b = divmod(n, NB)
                sp.wait_ge(message_ready, n + 1)
                sp.dma_start(message_table[b * P:b * P + rows[b], m * D:(m + 1) * D],
                             out_slots[0:rows[b], n % OUTS, :]).then_inc(messages_out[n % OUTS], 16)
                if b == NB // 2 and 2 <= m + 2 <= R:
                    sp.wait_ge(w_low, m + 1)
                    load_weights(m + 2)
            for n, v in enumerate((ln2_w, ln2_b)):
                sp.dma_start(ln2[:, n, :], v.partition_broadcast(P)).then_inc(ln2_in, 16)
            sp.wait_ge(self_biased, NB)
            sp.dma_start(bias_sb[:, :], b2.partition_broadcast(P)).then_inc(bias_in, 16)
            sp.wait_ge(ring_ready, G1)
            loads = [(256 * q, 256) for q in range(FFN_WORDS // 256)]
            while len(loads) < 3 * STEPS:
                at, words = loads.pop()
                loads += [(at, words // 2), (at + words // 2, words // 2)]
            for n, (at, words) in enumerate(loads):
                step = n // 3
                if n % 3 == 0 and step:
                    sp.wait_ge(ffn_in, 48 * step)
                    if step > 1:
                        sp.wait_ge(ffn_high_made, step - 1)
                if at < KD * F:
                    k, column = divmod(at, F)
                    source = w1[k * P:(k + 1) * P, column:column + words]
                else:
                    k, column = divmod(at - KD * F, D)
                    source = w2.rearrange("(p k) n -> p k n", p=P)[:, k, column:column + words]
                sp.dma_start(ffn_loaded[:, at:at + words], source).then_inc(ffn_in, 16)
            for b in range(NB):
                sp.wait_ge(y_ready, b + 1)
                sp.dma_start(out[b * P:b * P + rows[b], :], X[0:rows[b], b, :]).then_inc(out_done, 16)
            sp.wait_ge(out_done, 16 * NB)

        @block.gpsimd
        def _(pool):
            def iota(to, pattern, channel_multiplier):
                nc.gpsimd.iota(to, pattern, base=0, channel_multiplier=channel_multiplier,
                               allow_small_or_imprecise_dtypes=True)

            steps, norms = [0], [0]

            def done(ins):
                ins.then_inc(pool_step, 1)
                steps[0] += 1
                pool.wait_ge(pool_step, steps[0])

            def inverse_std(b):
                norms[0] += 1
                pool.wait_ge(var_ready, norms[0])
                done(nc.gpsimd.tensor_scalar(var_eps[:, b:b + 1], mv[:, b, 1:2], EPS, None, ALU.add))
                nc.gpsimd.tensor_tensor(rstd[:, b:b + 1], var_eps[:, b:b + 1], minus_half[:, :], ALU.pow
                                        ).then_inc(rstd_ready, 1)

            nc.gpsimd.memset(X[:, NB - 1, :], 0.0).then_inc(consts, 1)
            iota(iota_col[:, :], [[1, P]], 0)
            nc.gpsimd.memset(minus_half[:, :], -0.5)
            iota(index_p[:, :], [[P, 2]], 1)
            nc.gpsimd.memset(edge_data[:, :, :], 0.0)
            nc.gpsimd.memset(edge_block[:, :], -1.0)
            nc.gpsimd.memset(type_row[:, :], 0.0)
            nc.gpsimd.memset(row_f[:, :], 0.0)
            nc.gpsimd.memset(ones16[:, :], 1.0)
            nc.gpsimd.memset(ones32[:, :], 1.0).then_inc(consts, 1)
            iota(iota_rep[:, :, :], [[1, T], [0, RING]], 0)
            nc.gpsimd.memset(zeros16[:, :], 0.0)
            nc.gpsimd.memset(gidx[:, :], 0)
            nc.gpsimd.memset(segrow16[:, :], -1.0)
            nc.gpsimd.memset(HT[:, NB - 1:STEPS], 0.0)
            nc.gpsimd.memset(segrow[:, :], -1.0).then_inc(consts, 1)
            for b in range(NB):
                inverse_std(b)
            nc.gpsimd.memset(ACC[:, :, :], 0.0).then_inc(acc_clear, 1)
            done(nc.gpsimd.memset(gathered[:, :, :], 0.0))
            for s in range(RING):
                pool.sem_inc(slot_free[s], 1)
            pool.wait_ge(bias_in, 16)
            for b in range(NB):
                pool.wait_ge(norm_ready, b + 1)
                a = X[0:rows[b], b, :]
                nc.gpsimd.tensor_tensor(a, a, bias_sb[0:rows[b], :], ALU.add).then_inc(x_biased, 1)
            limits = [pool.to_reg(last_row[l]) for l in range(2)]
            turn_regs = [pool.alloc_register(f"turn{h}") for h in range(2)]
            staged_regs = [pool.alloc_register(f"staged{q}") for q in range(4)]
            for l in range(2):
                if l == 0:
                    table = [(parts_out[s], 16 * uses_of(s, PARTS, NB)) for s in range(PARTS)]
                else:
                    for b in range(NB):
                        inverse_std(b)
                    pool.wait_ge(ring_ready, S1)
                    table = [(messages_out[s], 16 * uses_of(s, OUTS, R * NB)) for s in range(OUTS)]
                for s, value in table:
                    pool.wait_ge(s, value)
                with pool.Fori(0, STEPS) as i:
                    turn, staged = [], []
                    for h in range(2):
                        pool.reg_alu(turn_regs[h], i * 2, l * HALVES + h + 1, ALU.add)
                        turn.append(pool.snap(turn_regs[h]))
                    for q in range(4):
                        pool.reg_alu(staged_regs[q], i * 4, l * STAGED + q + 1, ALU.add)
                        staged.append(pool.snap(staged_regs[q]))
                    for h in range(2):
                        for s in range(RING):
                            pool.wait_ge(*table[0])
                            pool.wait_ge(stage_ready, staged[2 * h + s // (RING // 2)])
                            pool.wait_ge(slot_free[s], turn[h])
                            nc.gpsimd.indirect_dma_start(
                                (gathered16, gathered)[l][:, s, :], None, gather_from[l],
                                bass.IndirectOffsetOnAxis(gidx_now[:, h, s:s + 1], 0),
                                bounds_check=limits[l], oob_is_err=False).then_inc(tile_in[s], 16)
            for part, b in ffn_order:
                if part == "w2" or (part == "x1" and b < NB):
                    inverse_std(b)

        @block.scalar
        def _(act):
            act.wait_ge(consts, 2)

            def relu(l, b):
                act.wait_ge(norm_ready, l * NB + b + 1)
                return nc.scalar.activation(H[:, b, :], H[:, b, :], ACT.Relu)

            def high_part(b):
                act.wait_ge(relu_ready, b + 1)
                if b >= PARTS:
                    act.wait_ge(parts_out[b % PARTS], 16)
                nc.scalar.activation(parts[:, b % PARTS, 0, :], H[:, b, :], ACT.Copy, scale=SPLIT
                                     ).then_inc(high_ready, 1)

            def copy_transposed(use, b):
                n = act_at[use]
                act.wait_ge(act_ready, n + 1)
                nc.scalar.copy(HT[:, b, :, 0:rows[b]],
                               act_ps[n % 2][:, :].rearrange("p (k n) -> p k n", k=KD)[:, :, 0:rows[b]]
                               ).then_inc(act_free, 1)

            def high_transposed(b):
                n = act_at[("t1", b)]
                act.wait_ge(act_ready, n + 1)
                nc.scalar.copy(h1_high[:, b, :, 0:rows[b]],
                               act_ps[n % 2][:, :].rearrange("p (k n) -> p k n", k=KD)[:, :, 0:rows[b]]
                               ).then_inc(h1_high_ready, 1)

            def split_weights(m):
                act.wait_ge(w_loaded_in[m % 2], 16 * (m // 2 + 1))
                if m >= 2:
                    act.wait_ge(ring_ready, M1 + (m - 1) * NB)
                nc.scalar.copy(w_parts[m % 2][:, 0], w_loaded[:, m % 2]).then_inc(w_high, 1)

            def permute_op(l, i, h):
                act.wait_ge(slot_made, i * 2 + (l * HALVES + h + 1))
                for c in range(BY_SCALAR[l]):
                    ins = nc.scalar.activation(seg_onehot[:, h, :, c], slot_onehot[:, h, :, c], ACT.Copy,
                                               scale=type_row[:, bass.ds(i * STEP + h * RING + c, 1)])
                if l:
                    for c in range(RING):
                        nc.scalar.activation(row_onehot[:, h, :, c], slot_onehot[:, h, :, c], ACT.Copy,
                                             scale=row_f[:, bass.ds(i * STEP + h * RING + c, 1)])
                    ins = nc.scalar.copy(mask_now[:, h], mask[:, :, bass.ds(i * STEP + h * RING, RING)])
                ins.then_inc(times_type_row, 1)

            def beside_gather(l):
                with act.Fori(0, STEPS) as i:
                    if l == 0:
                        act.wait_ge(alpha_done, i + 1)
                        nc.scalar.copy(h0_block[:, :, :], HT[:, bass.ds(i, 1), :, :].rearrange("p b k n -> p (b k) n")
                                       ).then_inc(h0_staged, 1)
                        for h in range(2):
                            permute_op(1, i, h)
                        act.wait_ge(alpha_done, i + 2)
                        nc.scalar.copy(H[:, bass.ds(i, 1), :], small_ps[:, :].unsqueeze(1)).then_inc(alpha_taken, 1)
                    for h in range(2 * (1 - l)):
                        act.wait_ge(slot_free[RING - 1], i * 2 + (l * HALVES + h + 2))
                        nc.scalar.copy(tile_counts[:, bass.ds(i * STEP + h * RING, RING)], act_ps[h][:, 0:RING]
                                       ).then_inc(counts_free, 1)
                    if l:
                        act.wait_ge(tile_in[0], i * 32 + 16 * (HALVES + 1))
                        act.wait_ge(ffn_in, i * 48 + 48)
                        nc.scalar.copy(ffn_high[:, bass.ds(i * PIECE, PIECE)], ffn_loaded[:, bass.ds(i * PIECE, PIECE)]
                                       ).then_inc(ffn_high_made, 1)

            for b in range(NB):
                relu(0, b).then_inc(relu_ready, 1)
            for b in range(PARTS):
                high_part(b)
            for b in range(NB):
                copy_transposed(("t0", b), b)
            for b in range(PARTS, NB):
                high_part(b)
            with act.Fori(0, STEPS) as i:
                for h in range(2):
                    permute_op(0, i, h)
            act.wait_ge(act_free, NB)
            act.wait_ge(consts, 4)
            beside_gather(0)
            split_weights(0)
            split_weights(1)
            for b in range(NB):
                relu(1, b).then_inc(relu_ready, 1)
                if b >= NB - 3:
                    high_transposed(b - NB + 3)
            for b in range(3, NB):
                high_transposed(b)
            for m in range(2, R + 1):
                split_weights(m)
            act.wait_ge(pad_clear, 1)
            act.wait_ge(tile_in[0], 16 * (HALVES + 1))
            beside_gather(1)
            act.wait_ge(rows_in, 16 * ROWS)
            for part, n in ffn_order:
                if part == "tx":
                    act.wait_ge(x1_transposed, n + 1)
                    nc.scalar.copy(x1_high[:, n].rearrange("p k n -> p (k n)"), x1_ps[n % 2][:, :]
                                   ).then_inc(x1_high_made, 1)
                elif part == "w1":
                    g, f = divmod(n, KF)
                    nodes = len(node_groups[g]) * P
                    act.wait_ge(mlp_ready, n + 1)
                    if n >= 2:
                        act.wait_ge(gelu_low_made, n - 1)
                    nc.scalar.activation(gelu[n % 2][:, 0:nodes], act_ps[n % 2][:, 0:nodes], ACT.Gelu,
                                         bias=b1_sb[:, f:f + 1]).then_inc(mlp_read, 1)
                    if g and f == 0:
                        act.wait_ge(ring_ready, F1 + node_groups[g][0])
                    act.wait_ge(mlp_read, n + 1)
                    nc.scalar.copy(gelu_high[:, f, 0:nodes], gelu[n % 2][:, 0:nodes]).then_inc(gelu_high_made, 1)

        @block.vector
        def _(dve):
            steps, norms, norm_of = [0], [0], {}

            def mark(ins):
                ins.then_inc(dve_step, 1)
                steps[0] += 1
                return steps[0]

            def done(ins):
                mark(ins)
                dve.wait_ge(dve_step, steps[0])

            def moments(of, b):
                done(nc.vector.bn_stats(stats[:, b, :], of[:, b, :]))
                measured(b, nc.vector.bn_aggr(mv[:, b, :], stats[:, b, :]))

            def measured(b, ins):
                ins.then_inc(var_ready, 1)
                norms[0] += 1
                norm_of[b] = norms[0]


            def normalise(of, b):
                dve.wait_ge(rstd_ready, norm_of[b])
                return nc.vector.tensor_scalar(H[:, b, :], of[:, b, :], mv[:, b, 0:1], rstd[:, b:b + 1],
                                               ALU.subtract, ALU.mult)

            def low_part(b):
                dve.wait_ge(high_ready, b + 1)
                nc.vector.scalar_tensor_tensor(out=parts[:, b % PARTS, 1, :], in0=H[:, b, :], scalar=SPLIT,
                                               in1=parts[:, b % PARTS, 0, :], op0=ALU.mult, op1=ALU.subtract
                                               ).then_inc(low_ready, 1)

            def low_weights(m):
                dve.wait_ge(w_high, m + 1)
                nc.vector.tensor_tensor(w_parts[m % 2][:, 1], w_loaded[:, m % 2], w_parts[m % 2][:, 0].bitcast(fp32),
                                        ALU.subtract).then_inc(w_low, 1)

            def low_transposed(b):
                n = act_at[("t1", b)]
                dve.wait_ge(h1_high_ready, b + 1)
                at = act_ps[n % 2][:, :].rearrange("p (k n) -> p k n", k=KD)[:, :, 0:rows[b]]
                nc.vector.tensor_tensor(h1_low[:, b, :, 0:rows[b]], at, h1_high[:, b, :, 0:rows[b]].bitcast(fp32),
                                        ALU.subtract).then_inc(act_free, 1)

            def layer_norm_0():
                for b in range(NB):
                    dve.wait_ge(x_in[b], 16)
                    moments(X, b)
                    if b:
                        normalise(X, b - 1).then_inc(norm_ready, 1)
                normalise(X, NB - 1).then_inc(norm_ready, 1)

            def rank_counts(l):
                seg, other = edges[0:EP, l, :], edges[0:EP, 1 - l, :]
                done(nc.vector.tensor_scalar(int_a[:, :], seg, 7, None, ALU.logical_shift_right))
                done(nc.vector.tensor_copy(edge_block[:, 0:EC], int_a[:, :]))
                mark(nc.vector.tensor_scalar(int_b[:, :], seg, P - 1, None, ALU.bitwise_and))
                mark(nc.vector.tensor_scalar(row_f[:, 0:EC] if l else edge_data[:, 2, 0:EC], other, 1.0, None, ALU.add))
                for k in range(NB):
                    mark(nc.vector.tensor_scalar(mask[:, k, :], edge_block[:, :], float(k), None, ALU.is_equal))
                dve.wait_ge(dve_step, steps[0])
                mark(nc.vector.tensor_scalar(edge_data[:, 3, 0:EC], int_b[:, :], 1.0, None, ALU.add))
                done(nc.vector.tensor_scalar(edge_f[:, :], int_b[:, :], 1.0, None, ALU.add))
                mark(nc.vector.scalar_tensor_tensor(out=type_row[:, 0:EC], in0=edges[0:EP, 2, :],
                                                    scalar=float(l << TYPE_AT), in1=edge_f[:, :], op0=ALU.mult,
                                                    op1=ALU.add))
                done(nc.vector.tensor_tensor_scan(seen2, ones32[0:EP, 0:1].to_broadcast([EP, NB * T]), mask2, 0.0,
                                                  ALU.mult, ALU.add))
                done(nc.vector.tensor_copy(last[:, :], seen[:, :, T - 1]))
                mark(nc.vector.tensor_copy(counts16[:, 0:1], last[:, 0:1]))
                nc.vector.tensor_tensor(counts16[:, 1:NB], last[:, 1:NB], last[:, 0:NB - 1], ALU.subtract).then_inc(
                    small_free, 1)

            def rank_places(l):
                dve.wait_ge(small_ready, 2 * l + 1)
                below, total = small_ps[0:EP, 0:NB], small_ps[:, NB:2 * NB]
                done(nc.vector.tensor_scalar(total_i[:, :], total, float(P - 1), None, ALU.add))
                done(nc.vector.tensor_scalar(total_i[:, :], total_i[:, :], 7, None, ALU.logical_shift_right))
                done(nc.vector.tensor_copy(tiles_of[:, 0, :], total_i[:, :]))
                done(nc.vector.tensor_tensor_scan(tiles_of[:, 1, :], ones32[:, 0:1].to_broadcast([P, NB]),
                                                  tiles_of[:, 0, :], 0.0, ALU.mult, ALU.add))
                done(nc.vector.tensor_tensor(tiles_of[:, 2, :], tiles_of[:, 1, :], tiles_of[:, 0, :], ALU.subtract))
                for c in range(2):
                    for n, m in ((0, 1), (1, 2)):
                        mark(nc.vector.tensor_scalar(reached[:, n, c, :], tiles_of[:, m, :], index_p[:, c:c + 1], None,
                                                     ALU.is_le))
                dve.wait_ge(dve_step, steps[0])
                mark(nc.vector.tensor_tensor(tile_key[:, l, :, :], reached[:, 1, :, :], reached[:, 0, :, :],
                                             ALU.subtract))
                done(nc.vector.tensor_reduce(key_col[:, :], reached[:, 0, :, :], AX.X, ALU.add))
                nc.vector.tensor_scalar(key_col[:, :], key_col[:, :], float(NB - 1), None, ALU.min).then_inc(small_free, 1)
                done(nc.vector.scalar_tensor_tensor(out=place0[:, :], in0=tiles_of[0:EP, 2, :], scalar=float(P),
                                                    in1=below, op0=ALU.mult, op1=ALU.add))
                done(nc.vector.tensor_scalar(place0[:, :], place0[:, :], -1.0, None, ALU.add))
                done(nc.vector.tensor_tensor(place0[:, 1:NB], place0[:, 1:NB], last[:, 0:NB - 1], ALU.subtract))
                nc.vector.sem_inc(small_free, 1)
                for k in range(NB):
                    mark(nc.vector.scalar_tensor_tensor(out=place[:, k, :], in0=seen[:, k, 0:EC],
                                                        scalar=place0[:, k:k + 1], in1=mask[:, k, 0:EC], op0=ALU.add,
                                                        op1=ALU.mult))
                dve.wait_ge(dve_step, steps[0])
                done(nc.vector.tensor_reduce(edge_f[:, :], place.rearrange("p k j -> p j k"), AX.X, ALU.add))
                done(nc.vector.tensor_copy(int_a[:, :], edge_f[:, :]))
                mark(nc.vector.tensor_scalar(int_b[:, :], int_a[:, :], 7, None, ALU.logical_shift_right))
                done(nc.vector.tensor_scalar(int_a[:, :], int_a[:, :], P - 1, None, ALU.bitwise_and))
                mark(nc.vector.tensor_copy(edge_data[:, 0, 0:EC], int_a[:, :]))
                done(nc.vector.tensor_copy(edge_data[:, 1, 0:EC], int_b[:, :]))

            def take_keys(l):
                dve.wait_ge(small_ready, 2 * l + 2)
                mark(nc.vector.tensor_copy(key_row[0:1, l, :], small_ps[0:1, 0:2 * P]))
                dve.wait_ge(dve_step, steps[0])
                nc.vector.sem_inc(small_free, 1)

            def permute_ops(l, i, h):
                def data(n, width):
                    return edge_data[:, n, bass.ds(i * STEP + h * RING, RING)].unsqueeze(1).to_broadcast(
                        [EP, width, RING])

                def by_slot():
                    dve.wait_ge(perm_used, i * 2 + (l * HALVES + h + 1))
                    nc.vector.tensor_tensor(slot_onehot[:, h], iota_rep[0:EP, 0:P, :], data(0, P), ALU.is_equal
                                            ).then_inc(slot_made, 1)

                def times_row():
                    dve.wait_ge(slot_made, i * 2 + (l * HALVES + h + 1))
                    nc.vector.tensor_tensor(row_onehot[:, h], slot_onehot[:, h], data(2, P), ALU.mult
                                            ).then_inc(perm_ready, 1)

                def times_type():
                    a = BY_SCALAR[l]
                    dve.wait_ge(slot_made, i * 2 + (l * HALVES + h + 1))
                    nc.vector.tensor_tensor(seg_onehot[:, h, :, a:RING], slot_onehot[:, h, :, a:RING],
                                            type_row[:, bass.ds(i * STEP + h * RING + a, RING - a)].unsqueeze(1)
                                            .to_broadcast([EP, P, RING - a]), ALU.mult)

                def by_tile():
                    nc.vector.tensor_tensor(tile_onehot[:, h], iota_rep[0:EP, :, :], data(1, T), ALU.is_equal)

                def by_segment_row():
                    nc.vector.tensor_tensor(count_onehot[:, h], iota_rep[0:EP, 1:P + 1, :], data(3, P), ALU.is_equal
                                            ).then_inc(perm_ready, 1)

                return [by_slot, by_tile] + ([by_segment_row] if l else [times_type, times_row])

            def lists(l):
                dve.wait_ge(perm_done, l + 1)
                row = gather_f[:, :]
                mark(nc.vector.tensor_scalar(row, perm_ps[:, 0:T], 0.0, 4096.0, ALU.is_equal, ALU.mult))
                done(nc.vector.tensor_copy(payload_i[:, 0, :], perm_ps[:, T:2 * T]))
                mark(nc.vector.tensor_scalar(payload_i[:, 1, :], payload_i[:, 0, :], TYPE_AT, None,
                                             ALU.logical_shift_right))
                done(nc.vector.tensor_scalar(payload_i[:, 0, :], payload_i[:, 0, :], 2 ** TYPE_AT - 1, None,
                                             ALU.bitwise_and))
                mark(nc.vector.tensor_scalar((segrow16, segrow)[l][:, 0:T], payload_i[:, 0, :], -1.0, None, ALU.add))
                done(nc.vector.scalar_tensor_tensor(out=row, in0=perm_ps[:, 0:T], scalar=-1.0, in1=row, op0=ALU.add,
                                                    op1=ALU.add))
                done(nc.vector.scalar_tensor_tensor(out=gidx[:, 0:T], in0=row, scalar=float((1, R)[l]),
                                                    in1=payload_i[:, 1, :], op0=ALU.mult, op1=ALU.add))
                if l:
                    done(nc.vector.tensor_scalar(inv[:, 1, :], perm_ps[:, 2 * T:2 * T + NB], 1.0, None, ALU.max))
                    done(nc.vector.reciprocal(inv[:, 1, :], inv[:, 1, :]))
                nc.vector.sem_inc(lists_ready, 1)

            def stage_indices(at, buf, s):
                nc.vector.tensor_copy(gidx_now[:, buf, s:s + RING // 2], gidx[:, bass.ds(at, RING // 2)]
                                      ).then_inc(stage_ready, 1)

            def segment_onehots(l, q, at, buf):
                if not (isinstance(q, int) and q == 0):
                    dve.wait_ge(slot_free[RING - 1], q)
                if l == 0:
                    ins = nc.vector.tensor_tensor(segment_onehot16[:, buf], iota_rep[:, 0:P, :],
                                                  segrow16[:, bass.ds(at, RING)].unsqueeze(1).to_broadcast(
                                                      [P, P, RING]), ALU.is_equal)
                else:
                    ins = nc.vector.tensor_tensor(segment_onehot[:, buf],
                                                  iota_col[:, :].unsqueeze(1).to_broadcast([P, RING, P]),
                                                  segrow[:, bass.ds(at, RING)].unsqueeze(2).to_broadcast(
                                                      [P, RING, P]), ALU.is_equal)
                ins.then_inc(onehot_ready, 1)

            def first_indices():
                stage_indices(0, 0, 0)
                stage_indices(RING // 2, 0, RING // 2)
                stage_indices(RING, 1, 0)

            regs = [dve.alloc_register(f"key{u}") for u in range(STEP)]

            EXTRA = [0, 1, 3, 6, 7, 9]
            HALVED = [u for u in range(STEP) if u not in EXTRA]

            def gather(l):
                with dve.Fori(0, STEPS) as i:
                    extra = permute_ops(1, i, 0) + permute_ops(1, i, 1)
                    for h in range(2):
                        stage_indices(i * STEP + (h + 1) * RING + RING // 2, 1 - h, RING // 2)
                        segment_onehots(l, i * 2 + (l * HALVES + h + 1), i * STEP + (h + 1) * RING, 1 - h)
                        half_regs = regs[h * RING:(h + 1) * RING]
                        dve.load(half_regs, key_row[0:1, l, bass.ds(i * STEP + h * RING, RING)])
                        keys = [dve.snap(r, min_val=0, max_val=NB - 1) for r in half_regs]
                        for s in range(RING):
                            u = h * RING + s
                            if s == RING // 2:
                                stage_indices(i * STEP + (h + 2) * RING, h, 0)
                            if l == 0 and u in EXTRA:
                                extra.pop(0)()
                            n = i * STEP + (GBASE[l] + u + 1)
                            dve.wait_ge(ring_ready, n)
                            bank = ring[(GBASE[l] + u) % 4]
                            halved = l == 1 or u in HALVED
                            if halved:
                                if l:
                                    dve.wait_ge(slot_free[(s - 1) % RING], i * 2 + (HALVES + h + 1 + (s > 0)))
                                elif u - 1 in HALVED:
                                    dve.wait_ge(half_added, i * len(HALVED) + HALVED.index(u))
                                else:
                                    dve.wait_ge(ring_free, n + 3)
                                a = ACC[:, bass.ds(keys[s], 1), 0:D // 2]
                                nc.vector.tensor_tensor(a, a, bank[:, 0:D // 2].unsqueeze(1), ALU.add
                                                        ).then_inc(slot_free[s] if l else half_added, 1)
                            dve.wait_ge(ring_free, n + 3)
                            first = D // 2 if halved else 0
                            a = ACC[:, bass.ds(keys[s], 1), first:D]
                            nc.vector.tensor_tensor(a, a, bank[:, first:D].unsqueeze(1), ALU.add
                                                    ).then_inc(ring_free, 1)
                    if l:
                        piece = bass.ds(i * PIECE, PIECE)
                        dve.wait_ge(ffn_high_made, i + 1)
                        nc.vector.tensor_tensor(ffn_low[:, piece], ffn_loaded[:, piece],
                                                ffn_high[:, piece].bitcast(fp32), ALU.subtract).then_inc(ffn_low_made, 1)

            def counts(l):
                dve.wait_ge(small_ready, 2 * l + 5)
                mark(nc.vector.tensor_copy(tile_counts_t[:, 0, :], small_ps[:, 0:P]))
                nc.vector.tensor_copy(tile_counts_t[0:T - P, 1, :], small_ps[0:T - P, P:2 * P]).then_inc(small_free, 1)
                dve.wait_ge(small_ready, 2 * l + 6)
                if l == 0:
                    r = rows[NB - 1]
                    done(nc.vector.memset(inv[:, 0, NB - 1:NB], 0.0))
                    mark(nc.vector.reciprocal(inv[:, 0, 0:NB - 1], small_ps[:, 0:NB - 1]))
                    done(nc.vector.reciprocal(inv[0:r, 0, NB - 1:NB], small_ps[0:r, NB - 1:NB]))
                    done(nc.vector.tensor_scalar(inv[:, 0, :], inv[:, 0, :], 1.0 / SPLIT, None, ALU.mult))

            dve.wait_ge(consts, 2)
            mark(nc.vector.tensor_scalar(ident[:, :], iota_col[:, :], index_p[:, 0:1], None, ALU.is_equal))
            done(nc.vector.tensor_scalar(upper16[:, :], iota_col[:, :], index_p[:, 0:1], None, ALU.is_gt))
            nc.vector.sem_inc(ring_free, 4)
            nc.vector.sem_inc(consts, 1)

            dve.wait_ge(edges_in, 96)
            rank_counts(0)
            layer_norm_0()
            rank_places(0)
            for b in range(NB):
                low_part(b)
            dve.wait_ge(consts, 4)
            with dve.Fori(0, STEPS) as i:
                for h in range(2):
                    for op in permute_ops(0, i, h):
                        op()
            take_keys(0)
            lists(0)
            first_indices()
            segment_onehots(0, 0, 0, 0)
            rank_counts(1)
            rank_places(1)
            take_keys(1)
            dve.wait_ge(acc_clear, 1)
            gather(0)
            counts(0)
            lists(1)
            dve.wait_ge(alpha_taken, STEPS + 1)
            dve.wait_ge(x_biased, NB)
            for b in range(NB):
                r = rows[b]
                dve.wait_ge(ring_ready, B0 + b + 1)
                nc.vector.scalar_tensor_tensor(out=X[0:r, b, :], in0=ring[(B0 + b) % 4][0:r, :],
                                               scalar=inv[0:r, 0, b:b + 1], in1=X[0:r, b, :], op0=ALU.mult, op1=ALU.add
                                               ).then_inc(ring_free, 1)
                dve.wait_ge(ring_free, 4 + B0 + b + 1)
                done(nc.vector.tensor_tensor(X[0:r, b, :], X[0:r, b, :], H[0:r, b, :], ALU.add))
                moments(X, b)
                if b:
                    normalise(X, b - 1).then_inc(norm_ready, 1)
                if b == NB // 2:
                    low_weights(0)
                if b == NB - 2:
                    low_transposed(0)
            normalise(X, NB - 1).then_inc(norm_ready, 1)
            low_transposed(1)
            dve.wait_ge(rows_in, 16 * ROWS)
            dve.wait_ge(bias_in, 32)
            for n in range(R * NB):
                m, b = divmod(n, NB)
                if n >= OUTS:
                    dve.wait_ge(messages_out[n % OUTS], 16 * (n // OUTS))
                dve.wait_ge(ring_ready, M1 + n + 1)
                nc.vector.tensor_tensor(out_slots[0:rows[b], n % OUTS, :], ring[(M1 + n) % 4][0:rows[b], :],
                                        relb_sb[0:rows[b], m, :], ALU.add).then_inc(ring_free, 1)
                dve.wait_ge(ring_free, 4 + M1 + n + 1)
                nc.vector.sem_inc(message_ready, 1)
                if m == 0:
                    if b + 2 < NB:
                        low_transposed(b + 2)
                    nc.vector.tensor_tensor(H[:, b, :], H[:, b, :], bias_sb[:, :], ALU.add).then_inc(self_biased, 1)
                if b == (0 if m else NB // 2) and m + 1 <= R:
                    low_weights(m + 1)
            first_indices()
            segment_onehots(1, HALVES + 1, 0, 0)
            dve.wait_ge(self_biased, NB)
            for b in range(NB):
                r = rows[b]
                dve.wait_ge(ring_ready, S1 + b + 1)
                nc.vector.tensor_tensor(H[0:r, b, :], H[0:r, b, :], ring[(S1 + b) % 4][0:r, :], ALU.add
                                        ).then_inc(ring_free, 1)
                mark(nc.vector.memset(ACC[:, (b - 1) % NB, :], 0.0))
            nc.vector.memset(ffn_loaded[:, FFN_WORDS:HELD], 0.0).then_inc(pad_clear, 1)
            dve.wait_ge(dve_step, steps[0])
            gather(1)

            def weighted_norm(b, w):
                done(normalise(H, b))
                done(nc.vector.tensor_tensor(H[:, b, :], H[:, b, :], w[:, 0, :], ALU.mult))
                return nc.vector.tensor_tensor(H[:, b, :], H[:, b, :], w[:, 1, :], ALU.add)

            def x1_step(b):
                if b < NB:
                    nc.vector.scalar_tensor_tensor(out=H[:, b, :], in0=ACC[:, b, :], scalar=inv[:, 1, b:b + 1],
                                                   in1=H[:, b, :], op0=ALU.mult, op1=ALU.add).then_inc(acc_used, 1)
                    dve.wait_ge(acc_used, b + 1)
                    statistics = mark(nc.vector.bn_stats(stats[:, b, :], H[:, b, :]))
                if b:
                    normed = mark(normalise(H, b - 1))
                if b < NB:
                    dve.wait_ge(dve_step, statistics)
                    measured(b, nc.vector.bn_aggr(mv[:, b, :], stats[:, b, :]))
                if b:
                    dve.wait_ge(dve_step, normed)
                    done(nc.vector.tensor_tensor(H[:, b - 1, :], H[:, b - 1, :], ln1[:, 0, :], ALU.mult))
                    nc.vector.tensor_tensor(H[:, b - 1, :], H[:, b - 1, :], ln1[:, 1, :], ALU.add).then_inc(x1_ready, 1)

            def output(b):
                r = rows[b]
                done(weighted_norm(b, ln2))
                nc.vector.tensor_tensor(X[0:r, b, :], X[0:r, b, :], H[0:r, b, :], ALU.add).then_inc(y_ready, 1)

            for part, n in ffn_order:
                if part == "x1":
                    x1_step(n)
                elif part == "tx":
                    dve.wait_ge(x1_high_made, n + 1)
                    nc.vector.tensor_tensor(x1_low[:, n].rearrange("p k n -> p (k n)"), x1_ps[n % 2][:, :],
                                            x1_high[:, n].rearrange("p k n -> p (k n)").bitcast(fp32), ALU.subtract
                                            ).then_inc(x1_low_made, 1)
                elif part == "w1":
                    g, f = divmod(n, KF)
                    nodes = len(node_groups[g]) * P
                    dve.wait_ge(gelu_high_made, n + 1)
                    nc.vector.tensor_tensor(gelu_low[:, f, 0:nodes], gelu[n % 2][:, 0:nodes],
                                            gelu_high[:, f, 0:nodes].bitcast(fp32), ALU.subtract
                                            ).then_inc(gelu_low_made, 1)
                else:
                    r = rows[n]
                    if n == 0:
                        dve.wait_ge(bias_in, 48)
                        dve.wait_ge(ln2_in, 32)
                    done(nc.vector.tensor_tensor(H[:, n, :], H[:, n, :], bias_sb[:, :], ALU.add))
                    dve.wait_ge(ring_ready, F1 + n + 1)
                    nc.vector.tensor_tensor(H[0:r, n, :], H[0:r, n, :], ring[(F1 + n) % 4][0:r, :], ALU.add
                                            ).then_inc(ring_free, 1)
                    dve.wait_ge(ring_free, 4 + F1 + n + 1)
                    moments(H, n)
                    if n:
                        output(n - 1)
            output(NB - 1)

        @block.tensor
        def _(pe):
            pe.wait_ge(consts, 4)

            def mm(*a, **k):
                return nc.tensor.matmul(*a, **k)

            def act_bank(n):
                if n >= 2:
                    pe.wait_ge(act_free, n - 1)
                return act_ps[n % 2]

            def transposes(use, b, ready, value):
                n = act_at[use]
                pe.wait_ge(ready, value)
                bank = act_bank(n)
                for k in range(KD):
                    ins = nc.tensor.transpose(bank[:, k * P:k * P + rows[b]], H[0:rows[b], b, k * P:(k + 1) * P],
                                              ident[0:rows[b], 0:rows[b]])
                ins.then_inc(act_ready, 1)

            def products(bank, b, terms):
                for m, (left, right) in enumerate(terms):
                    ins = mm(bank[0:rows[b], :], left, right, start=(m == 0), stop=(m == len(terms) - 1))
                return ins

            def node_product(n, b, terms):
                pe.wait_ge(ring_free, n + 1)
                products(ring[n % 4], b, terms).then_inc(ring_ready, 1)

            def of_block(b, w):
                return [(HT[:, b, k, 0:rows[b]], w[:, k, :]) for k in range(KD)]

            def alpha_term(i, k):
                if k == 0:
                    pe.wait_ge(h0_staged, i + 1)
                    pe.wait_ge(alpha_taken, i + 1)
                ins = mm(small_ps[:, :], h0_block[:, k, :], wa[:, k, :], start=(k == 0), stop=(k == KD - 1))
                if k == KD - 1:
                    ins.then_inc(alpha_done, 1)

            def rank_counts(l):
                pe.wait_ge(small_free, 4 * l + 1)
                mm(small_ps[0:EP, 0:NB], upper16[0:EP, 0:EP], counts16[:, :], start=True, stop=True)
                mm(small_ps[:, NB:2 * NB], ones16[0:EP, :], counts16[:, :], start=True, stop=True
                   ).then_inc(small_ready, 1)

            def key_rows(l):
                pe.wait_ge(small_free, 4 * l + 3)
                for c in range(2):
                    ins = mm(small_ps[0:1, c * P:(c + 1) * P], key_col[:, c:c + 1], ident[:, :], start=True, stop=True)
                ins.then_inc(small_ready, 1)

            def permute_zeros(l, first):
                if first and l:
                    pe.wait_ge(lists_ready, l)
                width = 2 * T + NB * l
                return mm(perm_ps[:, 0:width], zeros16[0:EP, 0:P], zeros16[0:EP, 0:width], start=first, stop=not first)

            def permute_column(l, i, h, c):
                if c == 0:
                    pe.wait_ge(perm_ready, i * 2 + (l * HALVES + h + 1))
                    pe.wait_ge(times_type_row, i * 2 + (l * HALVES + h + 1))
                mm(perm_ps[:, 0:T], row_onehot[:, h, :, c], tile_onehot[:, h, :, c], start=False, stop=False)
                ins = mm(perm_ps[:, T:2 * T], seg_onehot[:, h, :, c], tile_onehot[:, h, :, c], start=False, stop=False)
                if l:
                    ins = mm(perm_ps[:, 2 * T:2 * T + NB], count_onehot[:, h, :, c], mask_now[:, h, :, c], start=False,
                             stop=False)
                if c == RING - 1:
                    ins.then_inc(perm_used, 1)

            def gather(l):
                with pe.Fori(0, STEPS) as i:
                    half = [pe.snap(i * 2 + (l * HALVES + h + 1)) for h in range(2)]
                    arrived = [pe.snap(i * 32 + 16 * (l * HALVES + h + 1)) for h in range(2)]
                    for h in range(2):
                        pe.wait_ge(onehot_ready, half[h] + l)
                        if l == 0:
                            pe.wait_ge(counts_free, half[h])
                        for s in range(RING):
                            u = h * RING + s
                            pe.wait_ge(tile_in[s], arrived[h])
                            pe.wait_ge(ring_free, i * STEP + (GBASE[l] + u + 1))
                            bank = ring[(GBASE[l] + u) % 4]
                            if l == 0:
                                onehot = segment_onehot16[:, h, :, s]
                                for k in range(KD):
                                    for part in range(2):
                                        ins = mm(bank[:, k * P:(k + 1) * P],
                                                 gathered16[:, s, part * D + k * P:part * D + (k + 1) * P], onehot,
                                                 start=(part == 0), stop=(part == 1))
                            else:
                                onehot = segment_onehot[:, h, s, :]
                                ins = mm(bank[:, :], onehot, gathered[:, s, :], start=True, stop=True)
                            ins.then_inc(ring_ready, 1)
                            if l == 0:
                                mm(act_ps[h][:, s:s + 1], onehot, ones16[:, 0:1], start=True, stop=True
                                   ).then_inc(slot_free[s], 1)
                            if l == 0 and u % 2 == 0 and u < 2 * KD:
                                alpha_term(i, u // 2)
                            if l == 0 and u >= RING:
                                for c in range(2 * (u - RING), 2 * (u - RING) + 2):
                                    permute_column(1, i, c // RING, c % RING)

            def counts(l):
                pe.wait_ge(counts_free, 2 + HALVES * (l + 1))
                pe.wait_ge(small_free, l + 8)
                pe.wait_ge(alpha_taken, STEPS + 1)
                nc.tensor.transpose(small_ps[:, 0:P], tile_counts[:, 0:P], ident[:, :])
                nc.tensor.transpose(small_ps[0:T - P, P:2 * P], tile_counts[:, P:T], ident[:, :]).then_inc(small_ready, 1)

            def counts_by_key(l):
                pe.wait_ge(small_free, l + 9)
                for c, t in ((0, P), (1, T - P)):
                    ins = mm(small_ps[:, 0:NB], tile_counts_t[0:t, c, :], tile_key[0:t, l, c, :], start=(c == 0),
                             stop=(c == 1))
                ins.then_inc(small_ready, 1)

            def t1(b):
                transposes(("t1", b), b, relu_ready, NB + b + 1)

            def t0(b):
                transposes(("t0", b), b, relu_ready, b + 1)

            pe.sem_inc(perm_used, 2)
            pe.sem_inc(counts_free, 2)
            rank_counts(0)
            for b in range(NB):
                t0(b)
            key_rows(0)
            permute_zeros(0, True)
            with pe.Fori(0, STEPS) as i:
                for h in range(2):
                    for c in range(RING):
                        permute_column(0, i, h, c)
            permute_zeros(0, False).then_inc(perm_done, 1)
            rank_counts(1)
            key_rows(1)
            permute_zeros(1, True)
            pe.wait_ge(act_free, act_at[("t0", NB - 1)] + 1)
            pe.wait_ge(wa_in, 16)
            pe.wait_ge(small_free, 8)
            pe.sem_inc(alpha_done, 1)
            pe.sem_inc(alpha_taken, 1)
            gather(0)
            permute_zeros(1, False).then_inc(perm_done, 1)
            counts(0)
            counts_by_key(0)
            pe.wait_ge(wb_in, 16)
            pe.wait_ge(ring_free, 4 + B0)
            for b in range(NB):
                if b == NB - 1:
                    t1(0)
                node_product(B0 + b, b, [(ACC[:, b, k * P:k * P + rows[b]], wb[:, k, :]) for k in range(KD)])
            t1(1)
            for m in range(R + 1):
                pe.wait_ge(w_low, m + 1)
                for b in range(NB):
                    if m == 0:
                        pe.wait_ge(act_free, act_at[("t1", b)] + 1)
                    terms = []
                    for k in range(KD):
                        high, low = (h[:, b, k, 0:rows[b]] for h in (h1_high, h1_low))
                        w_of = [w_parts[m % 2][:, part, k, :] for part in range(2)]
                        terms += [(high, w_of[0]), (high, w_of[1]), (low, w_of[0])]
                    node_product(M1 + m * NB + b, b, terms)
                    if m == 0 and b + 2 < NB:
                        t1(b + 2)
            gather(1)
            pe.wait_ge(ffn_low_made, STEPS)
            for part, n in ffn_order:
                if part == "tx":
                    pe.wait_ge(x1_ready, n + 1)
                    if n >= 2:
                        pe.wait_ge(x1_low_made, n - 1)
                    for k in range(KD):
                        ins = nc.tensor.transpose(x1_ps[n % 2][:, k * P:(k + 1) * P], H[:, n, k * P:(k + 1) * P],
                                                  ident[:, :])
                    ins.then_inc(x1_transposed, 1)
                elif part == "w1":
                    g, f = divmod(n, KF)
                    a, b = node_groups[g][0], node_groups[g][-1] + 1
                    if f == 0:
                        pe.wait_ge(x1_low_made, b)
                    if n >= 2:
                        pe.wait_ge(mlp_read, n - 1)
                    terms = []
                    for k in range(KD):
                        high, low = (w[:, k, f::KF] for w in w1_parts)
                        terms += [(high, x1_high[:, a:b, k, :]), (high, x1_low[:, a:b, k, :]),
                                  (low, x1_high[:, a:b, k, :])]
                    for m, (left, right) in enumerate(terms):
                        ins = mm(act_ps[n % 2][:, 0:(b - a) * P], left, right, start=(m == 0), stop=(m == len(terms) - 1))
                    ins.then_inc(mlp_ready, 1)
                elif part == "w2":
                    g = group_of[n]
                    at = (n - node_groups[g][0]) * P
                    pe.wait_ge(ring_free, F1 + n + 1)
                    for f in range(KF):
                        if at == 0:
                            pe.wait_ge(gelu_low_made, g * KF + f + 1)
                        high, low = (w[:, f, at:at + rows[n]] for w in (gelu_high, gelu_low))
                        terms = [(high, w2_parts[0][:, f, :]), (high, w2_parts[1][:, f, :]), (low, w2_parts[0][:, f, :])]
                        for m, (left, right) in enumerate(terms):
                            ins = mm(ring[(F1 + n) % 4][0:rows[n], :], left, right, start=(f == 0 and m == 0),
                                     stop=(f == KF - 1 and m == len(terms) - 1))
                    ins.then_inc(ring_ready, 1)


_INS = ['x', 'src', 'dst', 'edge_type_4', 'L0_gnn_wc', 'L0_gnn_wn', 'L0_gnn_bias', 'L1_gnn_self_W', 'L1_gnn_self_b',
        'L1_gnn_rel_W', 'L1_gnn_rel_b', 'L1_gnn_ln1_w', 'L1_gnn_ln1_b', 'L1_gnn_W1', 'L1_gnn_b1', 'L1_gnn_W2',
        'L1_gnn_b2', 'L1_gnn_ln2_w', 'L1_gnn_ln2_b']


def kernel(**inputs):
    import numpy as _np
    import concourse.bacc as _bacc
    from concourse import mybir as _mybir
    from concourse.bass_utils import run_bass_kernel_spmd as _run

    nc = _bacc.Bacc("TRN2", target_bir_lowering=False, num_devices=1)
    arrays, args = {}, []
    for name in _INS:
        a = _np.ascontiguousarray(inputs[name])
        arrays[f"in_{name}_dram"] = a
        args.append(nc.dram_tensor(f"in_{name}_dram", a.shape, _mybir.dt.from_np(a.dtype), kind="ExternalInput").ap())
    shape = inputs['x'].shape
    args.append(nc.dram_tensor("out_0_dram", shape, _mybir.dt.float32, kind="ExternalOutput").ap())
    build_gnn(nc, *args)
    r = _run(nc, [arrays], core_ids=[0])
    return r.results[0]["out_0_dram"]
```
